# Optimizing a Trainium2 kernel written in Bass

```python
import numpy as np
import jax
import jax.numpy as jnp

def _softmax(x, axis=-1):
    return jax.nn.softmax(x, axis=axis)

def _gelu(x):
    return jax.nn.gelu(x, approximate=True)

def _silu(x):
    return jax.nn.silu(x)

def _sigmoid(x):
    return jax.nn.sigmoid(x)

def _layernorm(x, axis=-1, eps=1e-05):
    m = jnp.mean(x, axis=axis, keepdims=True)
    v = jnp.var(x, axis=axis, keepdims=True)
    return (x - m) / jnp.sqrt(v + eps)

def _scatter_add(tgt, idx, src, axis=0):
    return tgt.at[idx].add(src)

def _segment_sum(src, seg, n):
    return jax.ops.segment_sum(src, seg, n)
kernel_name = 'mk_vit_tower_d1_tok_img768_r4_075182'

def setup_inputs(seed: int=0):
    np.random.seed(seed)
    _w = jnp.asarray

    def _rec_inputs():
        import jax
        import jax.numpy as jnp
        _rk = jax.random.key(seed)
        x = -0.00016672 + 0.999947 * jax.random.normal(jax.random.fold_in(_rk, 1), (16, 3, 112, 112), jnp.float32)
        return x
    x = _rec_inputs()

    def _L0_tok_setup():
        import jax, jax.numpy as jnp
        import numpy as np
        P1, P2 = (16, 16)
        EMBED = 192

        def _patchify(images):
            B, C, H, W = images.shape
            h, w = (H // P1, W // P2)
            x = images.reshape(B, C, h, P1, w, P2)
            x = x.transpose(0, 2, 4, 3, 5, 1)
            return x.reshape(B, h * w, P1 * P2 * C)
        key = jax.random.key(seed)
        k1, k2, k3 = jax.random.split(key, 3)
        B, C, H, W = (64, 3, 96, 96)
        images = jax.random.normal(k1, (B, C, H, W), dtype=jnp.float32)
        patch_dim = P1 * P2 * C
        bound = 1.0 / np.sqrt(patch_dim)
        W_lin = jax.random.uniform(k2, (EMBED, patch_dim), minval=-bound, maxval=bound, dtype=jnp.float32)
        b_lin = jax.random.uniform(k3, (EMBED,), minval=-bound, maxval=bound, dtype=jnp.float32)
        return {'images': images, 'W_lin': W_lin, 'b_lin': b_lin}
    _L0_tok_all = _L0_tok_setup()
    _L0_tok_in = {k: v for k, v in _L0_tok_all.items() if k in ('W_lin', 'b_lin')}
    del _L0_tok_all

    def _L0_attn_setup():
        import jax, jax.numpy as jnp
        import numpy as np
        B, N, DIM, H = (8, 1024, 192, 12)
        HD = DIM // H
        SCALE = HD ** (-0.5)
        key = jax.random.key(seed)
        ks = jax.random.split(key, 6)
        x = jax.random.normal(ks[0], (B, N, DIM), dtype=jnp.float32)
        Wqkv = jax.random.normal(ks[1], (3 * DIM, DIM), dtype=jnp.float32) * DIM ** (-0.5)
        Wp = jax.random.normal(ks[2], (DIM, DIM), dtype=jnp.float32) * DIM ** (-0.5)
        bp = jnp.zeros((DIM,), dtype=jnp.float32)
        w_q = jax.random.normal(ks[3], (H, HD), dtype=jnp.float32)
        w_k = jax.random.normal(ks[4], (H, HD), dtype=jnp.float32)
        return {'x': x, 'Wqkv': Wqkv, 'Wp': Wp, 'bp': bp, 'w_q': w_q, 'w_k': w_k}
    _L0_attn_all = _L0_attn_setup()
    _L0_attn_in = {k: v for k, v in _L0_attn_all.items() if k in ('Wqkv', 'Wp', 'bp', 'w_q', 'w_k')}
    del _L0_attn_all

    def _L0_ffn_setup():
        import jax, jax.numpy as jnp
        import numpy as np
        NUM_EXPERTS = 8
        TOP_K = 2
        CAPACITY_FACTOR = 1.25
        MAX_GROUP_SIZE = 1024
        MIN_EXPERT_CAPACITY = 4

        def _moe_forward(x, w_router, wi, wo):
            B, T, D = x.shape
            E = NUM_EXPERTS
            num_tokens = B * T
            G = max(num_tokens // MAX_GROUP_SIZE, E)
            while num_tokens % G != 0 or G % E != 0:
                G += 1
            S = num_tokens // G
            C = max(int(TOP_K * CAPACITY_FACTOR * S / E), MIN_EXPERT_CAPACITY)
            xg = x.reshape(G, S, D)
            logits = jnp.einsum('gsd,de->gse', xg.astype(jnp.float32), w_router.astype(jnp.float32))
            probs = jax.nn.softmax(logits, axis=-1)
            gate, idx = jax.lax.top_k(probs, TOP_K)
            idx_kf = jnp.swapaxes(idx, 1, 2).reshape(G, TOP_K * S)
            mask = jax.nn.one_hot(idx_kf, E, dtype=jnp.int32)
            prio = jnp.cumsum(mask, axis=1) * mask - 1
            prio = jnp.swapaxes(prio.reshape(G, TOP_K, S, E), 1, 2)
            prio_se = prio.max(axis=2)
            gate_se = jnp.einsum('gsk,gske->gse', gate, jax.nn.one_hot(idx, E, dtype=gate.dtype))
            dispatch = jax.nn.one_hot(prio_se, C, dtype=x.dtype)
            combine = dispatch * gate_se[..., None].astype(x.dtype)
            expert_in = jnp.einsum('gsec,gsd->egcd', dispatch, xg)
            h = jax.nn.relu(jnp.einsum('egcd,edf->egcf', expert_in, wi))
            expert_out = jnp.einsum('egcf,efd->egcd', h, wo)
            out = jnp.einsum('gsec,egcd->gsd', combine, expert_out)
            return out.reshape(B, T, D)
        key = jax.random.key(seed)
        k1, k2, k3, k4 = jax.random.split(key, 4)
        B, T, D, F = (8, 256, 192, 768)
        x = jax.random.normal(k1, (B, T, D), jnp.float32)
        w_router = jax.random.normal(k2, (D, NUM_EXPERTS), jnp.float32) * D ** (-0.5)
        wi = jax.random.normal(k3, (NUM_EXPERTS, D, F), jnp.float32) * D ** (-0.5)
        wo = jax.random.normal(k4, (NUM_EXPERTS, F, D), jnp.float32) * F ** (-0.5)
        return {'x': x, 'w_router': w_router, 'wi': wi, 'wo': wo}
    _L0_ffn_all = _L0_ffn_setup()
    _L0_ffn_in = {k: v for k, v in _L0_ffn_all.items() if k in ('w_router', 'wi', 'wo')}
    del _L0_ffn_all
    return {'x': x, 'L0_tok_W_lin': _L0_tok_in['W_lin'], 'L0_tok_b_lin': _L0_tok_in['b_lin'], 'L0_attn_Wqkv': _L0_attn_in['Wqkv'], 'L0_attn_Wp': _L0_attn_in['Wp'], 'L0_attn_bp': _L0_attn_in['bp'], 'L0_attn_w_q': _L0_attn_in['w_q'], 'L0_attn_w_k': _L0_attn_in['w_k'], 'L0_ffn_w_router': _L0_ffn_in['w_router'], 'L0_ffn_wi': _L0_ffn_in['wi'], 'L0_ffn_wo': _L0_ffn_in['wo']}

def reference(x, L0_tok_W_lin, L0_tok_b_lin, L0_attn_Wqkv, L0_attn_Wp, L0_attn_bp, L0_attn_w_q, L0_attn_w_k, L0_ffn_w_router, L0_ffn_wi, L0_ffn_wo):
    import jax
    import jax.numpy as jnp

    def _L0_tok_ref(images, W_lin, b_lin):
        import jax, jax.numpy as jnp
        import numpy as np
        P1, P2 = (16, 16)
        EMBED = 192

        def _patchify(images):
            B, C, H, W = images.shape
            h, w = (H // P1, W // P2)
            x = images.reshape(B, C, h, P1, w, P2)
            x = x.transpose(0, 2, 4, 3, 5, 1)
            return x.reshape(B, h * w, P1 * P2 * C)
        patches = _patchify(images)
        return jnp.einsum('bnd,ed->bne', patches, W_lin) + b_lin

    def _L0_attn_ref(x, Wqkv, Wp, bp, w_q, w_k):
        import jax, jax.numpy as jnp
        import numpy as np
        B, N, DIM, H = (8, 1024, 192, 12)
        HD = DIM // H
        SCALE = HD ** (-0.5)
        b, n, c = x.shape
        qkv = x @ Wqkv.T
        qkv = qkv.reshape(b, n, 3, H, HD).transpose(2, 0, 3, 1, 4)
        q, k, v = (qkv[0], qkv[1], qkv[2])
        alpha = jnp.einsum('bhnc,hc->bhn', q, w_q) * SCALE
        alpha = jax.nn.softmax(alpha, axis=-1)
        global_q = jnp.einsum('bhn,bhnc->bhc', alpha, q)
        p = global_q[:, :, None, :] * k
        beta = jnp.einsum('bhnc,hc->bhn', p, w_k) * SCALE
        beta = jax.nn.softmax(beta, axis=-1)
        global_k = jnp.einsum('bhn,bhnc->bhc', beta, k)
        u = global_k[:, :, None, :] * v
        q_flat = q.transpose(0, 2, 1, 3).reshape(b, n, c)
        u_flat = u.transpose(0, 2, 1, 3).reshape(b, n, c)
        return u_flat @ Wp.T + bp + q_flat

    def _L0_ffn_ref(x, w_router, wi, wo):
        import jax, jax.numpy as jnp
        import numpy as np
        NUM_EXPERTS = 8
        TOP_K = 2
        CAPACITY_FACTOR = 1.25
        MAX_GROUP_SIZE = 1024
        MIN_EXPERT_CAPACITY = 4

        def _moe_forward(x, w_router, wi, wo):
            B, T, D = x.shape
            E = NUM_EXPERTS
            num_tokens = B * T
            G = max(num_tokens // MAX_GROUP_SIZE, E)
            while num_tokens % G != 0 or G % E != 0:
                G += 1
            S = num_tokens // G
            C = max(int(TOP_K * CAPACITY_FACTOR * S / E), MIN_EXPERT_CAPACITY)
            xg = x.reshape(G, S, D)
            logits = jnp.einsum('gsd,de->gse', xg.astype(jnp.float32), w_router.astype(jnp.float32))
            probs = jax.nn.softmax(logits, axis=-1)
            gate, idx = jax.lax.top_k(probs, TOP_K)
            idx_kf = jnp.swapaxes(idx, 1, 2).reshape(G, TOP_K * S)
            mask = jax.nn.one_hot(idx_kf, E, dtype=jnp.int32)
            prio = jnp.cumsum(mask, axis=1) * mask - 1
            prio = jnp.swapaxes(prio.reshape(G, TOP_K, S, E), 1, 2)
            prio_se = prio.max(axis=2)
            gate_se = jnp.einsum('gsk,gske->gse', gate, jax.nn.one_hot(idx, E, dtype=gate.dtype))
            dispatch = jax.nn.one_hot(prio_se, C, dtype=x.dtype)
            combine = dispatch * gate_se[..., None].astype(x.dtype)
            expert_in = jnp.einsum('gsec,gsd->egcd', dispatch, xg)
            h = jax.nn.relu(jnp.einsum('egcd,edf->egcf', expert_in, wi))
            expert_out = jnp.einsum('egcf,efd->egcd', h, wo)
            out = jnp.einsum('gsec,egcd->gsd', combine, expert_out)
            return out.reshape(B, T, D)
        return _moe_forward(x, w_router, wi, wo)
    h = _L0_tok_ref(x, L0_tok_W_lin, L0_tok_b_lin)
    h = h + _L0_attn_ref(_layernorm(h, axis=-1), L0_attn_Wqkv, L0_attn_Wp, L0_attn_bp, L0_attn_w_q, L0_attn_w_k)
    h = h + _L0_ffn_ref(_layernorm(h, axis=-1), L0_ffn_w_router, L0_ffn_wi, L0_ffn_wo)
    return h

_drawn_inputs = setup_inputs


def setup_inputs(seed=0):
    import zlib

    import numpy as np

    out = dict(_drawn_inputs(seed))
    spreads = {'L0_attn_bp': (0.0, 0.1)}
    factors = {}
    for name, (base, spread) in spreads.items():
        noise = np.random.default_rng([zlib.crc32(name.encode()), seed]).standard_normal(out[name].shape)
        drawn = base * np.exp(spread * noise) if base else spread * noise
        out[name] = jnp.asarray(drawn.astype(out[name].dtype))
    for name, factor in factors.items():
        out[name] = (out[name] * factor).astype(out[name].dtype)
    return out
```

```python
from contextlib import ExitStack

import numpy as np

import concourse.bass as bass
from concourse import mybir

F32 = mybir.dt.float32
F32R = mybir.dt.float32r
BF16 = mybir.dt.bfloat16
ALU = mybir.AluOpType
ACT = mybir.ActivationFunctionType
AX = mybir.AxisListType

IMAGES, N_TOK, D = 16, 49, 192
PATCH = 768
KT = PATCH // 128
HEADS, HD = 12, 16
SCALE = float(HD) ** -0.5
EPS = 1e-5
E, F, CAP = 8, 768, 30
G, S = 8, 98
GH = G // 2
TH = GH * S
DA, DB = 128, 64
FT = F // 128
HS = GH * CAP
SLOTS = G * CAP
EC = E * CAP

NB = 12
BANK_COLS = NB // 2 * N_TOK
A_COLS = 8 * N_TOK
B_COLS = 4 * N_TOK

QKV_J = DA + DB + DB + DB
QKV_W = D + 3 * QKV_J
SMALL = {}


def _place(name, width, at=[0]):
    SMALL[name] = (at[0], width)
    at[0] += width


_place("bias", D)
_place("mask", 128)
_place("wqk", 4)
_place("ident", 128)
_place("wp_a", D)
_place("wp_b", D)
_place("router_a", E)
_place("router_b", E)
_place("tri", S)
_place("ones", S)
_place("rank", GH * E)
_place("iota", CAP)
_place("eps", 2)
_place("power", 2)
SMALL_W = sum(w for _, w in SMALL.values())

WI_B = F
WO = F + F // 2
WEXP = WO + FT * D
WI_W = WO


def build(nc, x_in, wtok_in, wqkv_in, small_in, wexp_in, out):
    ctx = ExitStack()
    with ctx:
        def sb(name, shape, dt=F32, scope=ctx):
            return scope.enter_context(nc.sbuf_tensor(name, shape, dt))

        def sem(name):
            return ctx.enter_context(nc.semaphore(name))

        ps = ctx.enter_context(nc.psum_tensor("ps", [128, 8, 512], F32))

        small = sb("small", [128, SMALL_W])

        def const(name, rows=128):
            at, w = SMALL[name]
            return small[0:rows, at:at + w]

        tri = sb("tri", [S, S], BF16)
        ones = sb("ones", [S, S], BF16)
        blk = sb("blk", [128, 4, 128])
        h = sb("h", [S, G, D])
        xn = sb("xn", [S, G, D])
        stats = sb("stats", [S, G, 6])
        moments = sb("moments", [S, G, 2])
        var = sb("var", [S, G])
        rstd = sb("rstd", [S, G])
        xn2t_a = sb("xn2t_a", [128, G, S])
        xn2t_b = sb("xn2t_b", [DB, G, S])
        x_hi = sb("x_hi", [S, G, 256], F32R)
        x_lo = sb("x_lo", [S, G, 256], F32R)
        shifted = sb("shifted", [S, G, E])
        ex = sb("ex", [S, G, E])
        ex2 = sb("ex2", [S, G, E])
        ranked = sb("ranked", [S, G, E])
        ranked2 = sb("ranked2", [S, G, E])
        chosen = sb("chosen", [S, 2, 2, GH * E], BF16)
        slot2 = sb("slot2", [S, 2, 2, GH * E])
        slot = sb("slot", [S, 2, GH * E])
        gate = sb("gate", [S, 2, 3, GH * E])
        cols = sb("cols", [S, 2, 6, GH])
        disp = sb("disp", [S, G, EC], F32R)
        comb = sb("comb", [S, G, EC])
        ei = {(c, p): sb(f"ei_{c}_{p}", [128, E, SLOTS], F32R) for c in "ab" for p in ("hi", "lo")}
        raw = sb("raw", [128, 2, WEXP])
        w_hi = [sb(f"w_hi{i}", [128, WEXP], F32R) for i in range(2)]
        w_lo = [sb(f"w_lo{i}", [128, WEXP], F32R) for i in range(2)]

        early = ExitStack()
        x = sb("x", [128, 4, KT, 2 * S], F32, early)
        wtok = sb("wtok", [128, KT, D], F32, early)
        wqkv = sb("wqkv", [128, 2, QKV_W], F32, early)
        xnt_a = sb("xnt_a", [128, G * S], F32, early)
        xnt_b = sb("xnt_b", [DB + 1, G * S], F32, early)
        att = [{n: sb(f"{n}{half}", [128, NB, N_TOK], F32, early) for n in ("q", "k", "v", "e", "w")}
               for half in range(2)]
        acol = sb("acol", [128, 2, 2, 5, NB], F32, early)
        early.close()
        h_hi = [sb(f"h_hi{i}", [128, FT, SLOTS], F32R) for i in range(2)]
        h_lo = [sb(f"h_lo{i}", [128, FT, SLOTS], F32R) for i in range(2)]
        y = sb("y", [HS, 2, 2, D])
        y_all = sb("y_all", [HS, 2, G, D])
        res = sb("res", [S, G, D])
        combT = sb("combT", [HS, G, 2, S])

        x_loaded = [sem(f"x_loaded{c}") for c in range(4)]
        wtok_loaded = sem("wtok_loaded")
        small_loaded = sem("small_loaded")
        wqkv_loaded = sem("wqkv_loaded")
        ones_row = sem("ones_row")
        cast_ready = sem("cast_ready")
        blk_ready = sem("blk_ready")
        tok_ready = sem("tok_ready")
        added = sem("added")
        ln_stats = sem("ln_stats")
        ln_moments = sem("ln_moments")
        ln_var = sem("ln_var")
        ln_rstd = sem("ln_rstd")
        xn_ready = sem("xn_ready")
        tr_ready = sem("tr_ready")
        xnt_ready = sem("xnt_ready")
        proj_ready = {j: sem(f"{j}_ready") for j in "qkv"}
        proj_held = {j: sem(f"{j}_held") for j in "qkv"}
        att_logits = [sem(f"att_logits{a}") for a in (1, 2)]
        att_max = [sem(f"att_max{a}") for a in (1, 2)]
        att_shift = [sem(f"att_shift{a}") for a in (1, 2)]
        att_exp = [sem(f"att_exp{a}") for a in (1, 2)]
        att_sum = [sem(f"att_sum{a}") for a in (1, 2)]
        att_weighted = [sem(f"att_weighted{a}") for a in (1, 2)]
        att_wsum = [sem(f"att_wsum{a}") for a in (1, 2)]
        att_rsum = [sem(f"att_rsum{a}") for a in (1, 2)]
        att_glob = [sem(f"att_glob{a}") for a in (1, 2)]
        kq_ready = sem("kq_ready")
        u_ready = sem("u_ready")
        attn_out = sem("attn_out")
        tr2_ready = sem("tr2_ready")
        xn2t_ready = sem("xn2t_ready")
        router_ready = sem("router_ready")
        x_hi_ready = sem("x_hi_ready")
        x_lo_ready = sem("x_lo_ready")
        route_step = sem("route_step")
        route_exp = sem("route_exp")
        route_shift = sem("route_shift")
        first_ready = sem("first_ready")
        choice_ready = sem("choice_ready")
        cum_ready = sem("cum_ready")
        cum_used = sem("cum_used")
        slot_ready = sem("slot_ready")
        disp_ready = sem("disp_ready")
        rsum_ready = sem("rsum_ready")
        gate_step = sem("gate_step")
        comb_ready = sem("comb_ready")
        ei_psum = sem("ei_psum")
        ei_hi_ready = sem("ei_hi_ready")
        ei_lo_ready = sem("ei_lo_ready")
        combT_psum = sem("combT_psum")
        combT_ready = sem("combT_ready")
        wi_loaded = [sem(f"wi_loaded{i}") for i in range(2)]
        wo_loaded = [sem(f"wo_loaded{i}") for i in range(2)]
        wi_hi = sem("wi_hi")
        wi_lo = sem("wi_lo")
        wo_hi = sem("wo_hi")
        wo_lo = sem("wo_lo")
        hid_psum = sem("hid_psum")
        hid_hi = sem("hid_hi")
        hid_lo = sem("hid_lo")
        lower_rows = sem("lower_rows")
        y_psum = sem("y_psum")
        y_held = sem("y_held")
        y_moved = [sem(f"y_moved{i}") for i in range(2)]
        mix_psum = sem("mix_psum")
        res_ready = sem("res_ready")
        stored = sem("stored")

        block = ctx.enter_context(nc.Block())

        def blocks(bank):
            return ps[:, bank:bank + 2, 0:BANK_COLS].rearrange("p b (s n) -> p b s n", n=N_TOK)

        def halves(t):
            return t.rearrange("p (b s) n -> p b s n", b=2)

        def spread(col):
            return col.rearrange("p (b s) -> p b s", b=2).unsqueeze(3).broadcast_to([128, 2, NB // 2, N_TOK])

        Q_BANK, K_BANK, V_BANK = (6, 0), (0, 4), (2, 2)
        L_BANK = ((6, 0), (6, 0))
        OUT_BANK = (4, 2)
        TR2_BANK = 6
        DISP_BANK = (0, 4)

        @block.sync
        def _(sp):
            sp.dma_start(wtok[:].rearrange("p k d -> p (k d)"), wtok_in).then_inc(wtok_loaded, 16)
            sp.dma_start(x[:, 0], x_in[0]).then_inc(x_loaded[0], 16)
            sp.dma_start(small[:], small_in).then_inc(small_loaded, 16)
            sp.dma_start(x[:, 1], x_in[1]).then_inc(x_loaded[1], 16)
            sp.dma_start(x[:, 2], x_in[2]).then_inc(x_loaded[2], 16)
            sp.dma_start(x[:, 3], x_in[3]).then_inc(x_loaded[3], 16)
            sp.dma_start(wqkv[:].rearrange("p k d -> p (k d)"), wqkv_in).then_inc(wqkv_loaded, 16)

            def load_expert(e, ring):
                sp.dma_start(raw[:, ring, 0:WI_W], wexp_in[e, :, 0:WI_W]).then_inc(wi_loaded[ring], 16)
                sp.dma_start(raw[:, ring, WO:WEXP], wexp_in[e, :, WO:WEXP]).then_inc(wo_loaded[ring], 16)

            def move_y(e):
                sp.wait_ge(y_held, e + 1)
                for half in range(2):
                    dst = y_all[CAP * (e % 4):CAP * (e % 4) + CAP, e // 4, GH * half:GH * half + GH, :]
                    for g in range(GH):
                        sp.dma_start(dst[:, g, :], y[g * CAP:g * CAP + CAP, e % 2, half, :]).then_inc(y_moved[e % 2], 16)

            for e in range(2):
                load_expert(e, e)
            for e in range(2, E):
                sp.wait_ge(wi_hi, e - 1)
                sp.wait_ge(wi_lo, e - 1)
                sp.dma_start(raw[:, e % 2, 0:WI_W], wexp_in[e, :, 0:WI_W]).then_inc(wi_loaded[e % 2], 16)
                sp.wait_ge(wo_hi, e - 1)
                sp.wait_ge(wo_lo, e - 1)
                sp.dma_start(raw[:, e % 2, WO:WEXP], wexp_in[e, :, WO:WEXP]).then_inc(wo_loaded[e % 2], 16)
                if e >= 3:
                    move_y(e - 3)
            for e in range(E - 3, E):
                move_y(e)
            for g in range(G):
                sp.wait_ge(res_ready, g + 1)
                sp.dma_start(out[g * S:(g + 1) * S, :], res[:, g, :]).then_inc(stored, 16)
            sp.wait_ge(stored, 16 * G)

        @block.tensor
        def _(pe):
            def mm(o, a, b, first, last):
                return nc.tensor.matmul(o, a, b, start=first, stop=last)

            def mm3(o, a, b, first, last):
                mm(o, a[0], b[0], first, False)
                mm(o, a[0], b[1], False, False)
                return mm(o, a[1], b[0], False, last)

            def embed(g):
                if g % 2 == 0:
                    pe.wait_ge(x_loaded[g // 2], 16)
                if g >= 4:
                    pe.wait_ge(added, g - 3)
                for k in range(KT):
                    last = mm(ps[0:S, g % 4, 0:D], x[:, g // 2, k, (g % 2) * S:(g % 2) * S + S], wtok[:, k, :],
                              k == 0, k == KT - 1)
                last.then_inc(tok_ready, 1)

            def turn(g):
                pe.wait_ge(xn_ready, g + 1)
                if g >= 2:
                    pe.wait_ge(xnt_ready, g - 1)
                b = 4 + g % 2
                nc.tensor.transpose(ps[0:DA, b, 0:S], xn[:, g, 0:DA], const("ident", S)[:, 0:S])
                nc.tensor.transpose(ps[0:DB, b, 128:128 + S], xn[:, g, DA:D], const("ident", S)[:, 0:S]).then_inc(tr_ready, 1)

            def project(j, half):
                bank = (Q_BANK, K_BANK, V_BANK)["qkv".index(j)][half]
                pe.wait_ge(xnt_ready, GH * (half + 1))
                if half == 0 and j == "q":
                    pe.wait_ge(wqkv_loaded, 16)
                if (j, half) == ("k", 0) or (j, half) == ("v", 0):
                    pe.wait_ge(added, G)
                if (j, half) == ("q", 1):
                    pe.wait_ge(proj_held["k"], 1)
                if (j, half) == ("v", 1):
                    pe.wait_ge(proj_held["v"], 1)
                if (j, half) == ("k", 1):
                    pe.wait_ge(xnt_ready, G)
                w0 = D + QKV_J * "qkv".index(j)
                t0 = TH * half
                w_a = [wqkv[0:(DA, DB)[k], k, w0:w0 + 128] for k in range(2)]
                w_b_low = [wqkv[0:(DA, DB)[k], k, w0 + 192:w0 + 320] for k in range(2)]
                w_b_high = [wqkv[0:(DA, DB)[k], k, w0 + 128:w0 + 256] for k in range(2)]
                xk = (xnt_a, xnt_b[0:DB])
                for k in range(2):
                    mm(ps[:, bank, 0:BANK_COLS], w_a[k], xk[k][:, t0:t0 + BANK_COLS], k == 0, k == 1)
                for k in range(2):
                    mm(ps[:, bank + 1, 0:A_COLS - BANK_COLS], w_a[k], xk[k][:, t0 + BANK_COLS:t0 + A_COLS], k == 0, k == 1)
                o = ps[:, bank + 1, A_COLS - BANK_COLS:BANK_COLS]
                for k in range(2):
                    mm(o, w_b_low[k], xk[k][:, t0:t0 + B_COLS], k == 0, False)
                    last = mm(o, w_b_high[k], xk[k][:, t0 + B_COLS:t0 + 2 * B_COLS], False, k == 1)
                last.then_inc(proj_ready[j], 1)

            def logits(stage, half):
                bank = L_BANK[stage][half]
                if stage == 0:
                    pe.wait_ge(blk_ready, 4)
                    pe.wait_ge(proj_held["q"], half + 1)
                    src = att[half]["q"]
                else:
                    pe.wait_ge(att_shift[0], half + 1)
                    pe.wait_ge(kq_ready, half + 1)
                    src = att[half]["w"]
                src = src[:].rearrange("p s n -> p (s n)")
                mm(ps[:, bank, 0:BANK_COLS], blk[:, 2 * stage, :], src[:, 0:BANK_COLS], True, True)
                mm(ps[:, bank + 1, 0:A_COLS - BANK_COLS], blk[:, 2 * stage, :], src[:, BANK_COLS:A_COLS], True, True)
                mm(ps[:, bank + 1, A_COLS - BANK_COLS:BANK_COLS], blk[:, 2 * stage + 1, :], src[:, A_COLS:], True,
                   True).then_inc(att_logits[stage], 1)

            def acc(o, a, b, first, last):
                return nc.tensor.matmul(o, a, b, start=first, stop=last, skip_group_check=True)

            def residual_q(half):
                bank = OUT_BANK[half]
                pe.wait_ge(ones_row, 1)
                pe.wait_ge(proj_held["kv"[half]], 2)
                for g in range(GH):
                    o = ps[0:S, bank + g // 2, g % 2 * D:g % 2 * D + D]
                    t = (GH * half + g) * S
                    acc(o, xnt_a[:, t:t + S], wqkv[:, 0, 0:D], g % 2 == 0, False)
                    acc(o, xnt_b[:, t:t + S], wqkv[0:DB + 1, 1, 0:D], False, False)

            def attention_out(half):
                bank = OUT_BANK[half]
                pe.wait_ge(u_ready, half + 1)
                u = att[half]["w"][:].rearrange("p s n -> p (s n)")
                for g in range(GH):
                    o = ps[0:S, bank + g // 2, g % 2 * D:g % 2 * D + D]
                    acc(o, u[:, g * S:g * S + S], const("wp_a"), False, False)
                    r, c = DB * (g // 2), A_COLS + g % 2 * S
                    last = acc(o, u[r:r + DB, c:c + S], const("wp_b")[r:r + DB, :], False, g % 2 == 1)
                    if g % 2 == 1:
                        last.then_inc(attn_out, 1)

            def turn2(g):
                pe.wait_ge(xn_ready, G + g + 1)
                if g < 2:
                    pe.wait_ge(att_shift[1], 1)
                else:
                    pe.wait_ge(xn2t_ready, g - 1)
                b = TR2_BANK + g % 2
                nc.tensor.transpose(ps[0:DA, b, 0:S], xn[:, g, 0:DA], const("ident", S)[:, 0:S])
                nc.tensor.transpose(ps[0:DB, b, 128:128 + S], xn[:, g, DA:D], const("ident", S)[:, 0:S]).then_inc(tr2_ready, 1)

            def router(half):
                bank = OUT_BANK[half]
                for g in range(GH):
                    gg = GH * half + g
                    pe.wait_ge(xn2t_ready, gg + 1)
                    o = ps[0:S, bank, g * E:g * E + E]
                    mm(o, xn2t_a[:, gg, :], const("router_a"), True, False)
                    last = mm(o, xn2t_b[:, gg, :], const("router_b", DB), False, True)
                last.then_inc(router_ready, 1)

            def cumulate(half):
                bank = OUT_BANK[half] + 1
                pe.wait_ge(first_ready, half + 1)
                mm(ps[0:S, bank, 0:GH * E], tri[:], chosen[:, half, 0, :], True, True)
                mm(ps[0:S, bank, GH * E:2 * GH * E], ones[:], chosen[:, half, 0, :], True, False)
                pe.wait_ge(choice_ready, half + 1)
                mm(ps[0:S, bank, GH * E:2 * GH * E], tri[:], chosen[:, half, 1, :], False, True).then_inc(cum_ready, 1)

            def dispatch(g):
                if g % GH == 0:
                    pe.wait_ge(x_hi_ready, g // GH + 1)
                    pe.wait_ge(x_lo_ready, g // GH + 1)
                    if g == 0:
                        pe.wait_ge(att_shift[1], 2)
                pe.wait_ge(disp_ready, g // 2 + 1)
                bank = DISP_BANK[g % 2]
                if g == 1:
                    pe.wait_ge(cum_used, 1)
                if g >= 2:
                    pe.wait_ge(ei_lo_ready, 2 * (g - 1))
                for c in range(2):
                    mm(ps[:, bank + c, 0:EC], x_hi[:, g, c * 128:c * 128 + 128], disp[:, g, :], True, False)
                    mm(ps[:, bank + c, 0:EC], x_lo[:, g, c * 128:c * 128 + 128], disp[:, g, :], False,
                       True).then_inc(ei_psum, 1)

            def turn_comb(half):
                pe.wait_ge(comb_ready, half + 1)
                if half == 0:
                    pe.wait_ge(cum_used, 2)
                else:
                    pe.wait_ge(xn2t_ready, G)
                for q in range(4):
                    g, s = GH * half + q, 0
                    b = (2, 6)[half] + q // 2
                    for s in range(2):
                        c = (q % 2 * 2 + s) * 128
                        last = nc.tensor.transpose(ps[0:HS, b, c:c + S], comb[:, g, s * HS:s * HS + HS],
                                                   const("ident", S)[:, 0:S])
                last.then_inc(combT_psum, 1)

            def expert_in(e, buf):
                pe.wait_ge(wi_hi, e + 1)
                pe.wait_ge(wi_lo, e + 1)
                def from_a(f, o, first):
                    return mm3(o, [v[buf][:, f * 128:f * 128 + 128] for v in (w_hi, w_lo)],
                               [ei["a", p][:, e, :] for p in ("hi", "lo")], first, not first)

                def from_b(f, o, first):
                    r, c = DB * (f // 3), WI_B + f % 3 * 128
                    return mm3(o, [v[buf][r:r + DB, c:c + 128] for v in (w_hi, w_lo)],
                               [ei["b", p][r:r + DB, e, :] for p in ("hi", "lo")], first, not first)

                for pair in range(FT // 2):
                    o = [ps[:, 3 * buf + pair, t * SLOTS:t * SLOTS + SLOTS] for t in range(2)]
                    if pair == 1:
                        from_b(2, o[0], True).then_inc(lower_rows, 1)
                        from_a(2, o[0], False)
                        from_a(3, o[1], True)
                        pe.wait_ge(lower_rows, e + 1)
                        last = from_b(3, o[1], False)
                    else:
                        for t in range(2):
                            from_a(2 * pair + t, o[t], True)
                            last = from_b(2 * pair + t, o[t], False)
                    last.then_inc(hid_psum, 1)

            def expert_out(e, buf):
                pe.wait_ge(wo_hi, e + 1)
                pe.wait_ge(wo_lo, e + 1)
                pe.wait_ge(hid_hi, 3 * (e + 1))
                pe.wait_ge(hid_lo, 3 * (e + 1))
                for half in range(2):
                    o = ps[0:HS, 6 + buf, half * D:half * D + D]
                    for f in range(FT):
                        last = mm3(o, [v[buf][:, f, half * HS:half * HS + HS] for v in (h_hi, h_lo)],
                                   [v[buf][:, WO + f * D:WO + f * D + D] for v in (w_hi, w_lo)], f == 0, f == FT - 1)
                last.then_inc(y_psum, 1)

            def mix(quad, g):
                o = ps[0:S, g // 2, g % 2 * 256:g % 2 * 256 + D]
                last = acc(o, combT[:, g, quad, :], y_all[:, quad, g, :], quad == 0 and g % 2 == 0, quad == 1)
                if quad == 1 and g % 2 == 1:
                    last.then_inc(mix_psum, 1)

            pe.wait_ge(wtok_loaded, 16)
            for g in range(4):
                embed(g)
            pe.wait_ge(small_loaded, 16)
            for g in range(4):
                turn(g)
                embed(4 + g)
            project("q", 0)
            project("k", 0)
            project("v", 0)
            logits(0, 0)
            for g in range(4, 8):
                turn(g)
            project("q", 1)
            project("k", 1)
            logits(0, 1)
            project("v", 1)
            residual_q(0)
            logits(1, 0)
            residual_q(1)
            attention_out(0)
            logits(1, 1)
            for g in range(4):
                turn2(g)
            router(0)
            pe.wait_ge(cast_ready, 2)
            cumulate(0)
            attention_out(1)
            for g in range(4):
                dispatch(g)
            for g in range(4, 8):
                turn2(g)
            router(1)
            cumulate(1)
            for g in range(4, 8):
                dispatch(g)
            turn_comb(0)
            turn_comb(1)
            pe.wait_ge(combT_ready, 2)
            pe.wait_ge(ei_hi_ready, 2 * G)
            pe.wait_ge(ei_lo_ready, 2 * G)
            expert_in(0, 0)
            for e in range(E - 1):
                if e >= 1:
                    pe.wait_ge(hid_lo, 3 * e)
                expert_in(e + 1, (e + 1) % 2)
                if e >= 2:
                    pe.wait_ge(y_held, e - 1)
                expert_out(e, e % 2)
            pe.wait_ge(y_held, E - 2)
            expert_out(E - 1, (E - 1) % 2)
            pe.wait_ge(y_moved[0], 16 * 8 * 2)
            pe.wait_ge(y_moved[1], 16 * 8 * 2)
            for g in range(G):
                mix(0, g)
            pe.wait_ge(y_moved[0], 16 * 8 * 4)
            pe.wait_ge(y_moved[1], 16 * 8 * 4)
            for g in range(G):
                mix(1, g)

        @block.scalar
        def _(act):
            def copy_turned(g, ready, to_a, to_b, bank, done, count):
                act.wait_ge(ready, count)
                nc.scalar.activation(to_a, ps[0:DA, bank, 0:S], ACT.Copy)
                nc.scalar.activation(to_b, ps[0:DB, bank, 128:128 + S], ACT.Copy).then_inc(done, 1)

            def hold(j, half):
                bank = (Q_BANK, K_BANK, V_BANK)["qkv".index(j)][half]
                act.wait_ge(proj_ready[j], half + 1)
                nc.scalar.activation(halves(att[half][j][:]), blocks(bank), ACT.Copy).then_inc(proj_held[j], 1)

            def att_exps(stage, half):
                act.wait_ge(att_shift[stage], half + 1)
                e = att[half]["e"]
                nc.scalar.activation(e[:], e[:], ACT.Exp).then_inc(att_exp[stage], 1)

            def turned1(g):
                copy_turned(g, tr_ready, xnt_a[:, g * S:g * S + S], xnt_b[0:DB, g * S:g * S + S], 4 + g % 2, xnt_ready, g + 1)

            def turned2(g):
                copy_turned(g, tr2_ready, xn2t_a[:, g, :], xn2t_b[:, g, :], TR2_BANK + g % 2, xn2t_ready, g + 1)

            def split_x(half):
                act.wait_ge(xn_ready, G + GH * (half + 1))
                gs = slice(GH * half, GH * half + GH)
                nc.scalar.activation(x_hi[:, gs, 0:DA], xn[:, gs, 0:DA], ACT.Copy)
                for c in (DA, DA + DB):
                    last = nc.scalar.activation(x_hi[:, gs, c:c + DB], xn[:, gs, DA:D], ACT.Copy)
                last.then_inc(x_hi_ready, 1)

            def route_exps(half):
                act.wait_ge(route_shift, half + 1)
                gs = slice(GH * half, GH * half + GH)
                nc.scalar.activation(ex[:, gs, :], shifted[:, gs, :], ACT.Exp).then_inc(route_exp, 1)

            def slots_hi(g):
                bank = DISP_BANK[g % 2]
                for c in range(2):
                    act.wait_ge(ei_psum, 2 * g + c + 1)
                    dst = ei["ab"[c], "hi"][:, :, g * CAP:g * CAP + CAP]
                    src = ps[:, bank + c, 0:EC].rearrange("p (e c) -> p e c", e=E)
                    nc.scalar.activation(dst, src, ACT.Copy).then_inc(ei_hi_ready, 1)

            def split_in(e):
                act.wait_ge(wi_loaded[e % 2], 16 * (e // 2 + 1))
                if e >= 2:
                    act.wait_ge(hid_psum, 3 * (e - 1))
                nc.scalar.activation(w_hi[e % 2][:, 0:WI_W], raw[:, e % 2, 0:WI_W], ACT.Copy).then_inc(wi_hi, 1)

            def split_out(e):
                act.wait_ge(wo_loaded[e % 2], 16 * (e // 2 + 1))
                if e >= 2:
                    act.wait_ge(y_psum, e - 1)
                nc.scalar.activation(w_hi[e % 2][:, WO:WEXP], raw[:, e % 2, WO:WEXP], ACT.Copy).then_inc(wo_hi, 1)

            def hidden_hi(e):
                for pair in range(FT // 2):
                    act.wait_ge(hid_psum, 3 * e + pair + 1)
                    if e >= 2 and pair == 0:
                        act.wait_ge(y_psum, e - 1)
                    nc.scalar.activation(h_hi[e % 2][:, 2 * pair:2 * pair + 2, :],
                                         ps[:, 3 * (e % 2) + pair, 0:2 * SLOTS].rearrange("p (t s) -> p t s", t=2),
                                         ACT.Relu).then_inc(hid_hi, 1)

            for g in range(4):
                turned1(g)
            hold("q", 0)
            hold("k", 0)
            hold("v", 0)
            for g in range(4, 8):
                turned1(g)
            hold("q", 1)
            att_exps(0, 0)
            hold("k", 1)
            att_exps(0, 1)
            hold("v", 1)
            split_in(0)
            att_exps(1, 0)
            split_out(0)
            att_exps(1, 1)
            split_in(1)
            for g in range(4):
                turned2(g)
            split_x(0)
            route_exps(0)
            for g in range(4):
                slots_hi(g)
            for g in range(4, 8):
                turned2(g)
            split_x(1)
            route_exps(1)
            for g in range(4, 8):
                slots_hi(g)
            for half in range(2):
                act.wait_ge(combT_psum, half + 1)
                for q in range(2):
                    src = ps[0:HS, (2, 6)[half] + q, :].rearrange("p (g e s) -> p g e s", g=2, e=2)[:, :, :, 0:S]
                    last = nc.scalar.activation(combT[:, GH * half + 2 * q:GH * half + 2 * q + 2, :, :], src, ACT.Copy)
                last.then_inc(combT_ready, 1)
            hidden_hi(0)
            for e in range(E - 1):
                if e + 2 < E:
                    split_in(e + 2)
                hidden_hi(e + 1)
                split_out(e + 1)

        @block.vector
        def _(dve):
            def norm_pair(p, source):
                g0 = 2 * (p % GH)
                for i in range(2):
                    source(g0 + i, i)
                for i in range(2):
                    dve.wait_ge(added, 2 * p + i + 1)
                    nc.vector.bn_stats(stats[:, g0 + i, :], h[:, g0 + i, :]).then_inc(ln_stats, 1)
                for i in range(2):
                    dve.wait_ge(ln_stats, 2 * p + i + 1)
                    nc.vector.bn_aggr(moments[:, g0 + i, :], stats[:, g0 + i, :]).then_inc(ln_moments, 1)
                dve.wait_ge(ln_rstd, p + 1)
                for i in range(2):
                    g = g0 + i
                    nc.vector.tensor_scalar(xn[:, g, :], h[:, g, :], moments[:, g, 0:1], rstd[:, g:g + 1],
                                            ALU.subtract, ALU.mult).then_inc(xn_ready, 1)

            def embedded(g, i):
                dve.wait_ge(tok_ready, g + 1)
                nc.vector.tensor_tensor(h[:, g, :], ps[0:S, g % 4, 0:D], const("bias", S), ALU.add).then_inc(added, 1)

            def attended(g, i):
                dve.wait_ge(attn_out, g // 2 + 1)
                bank = OUT_BANK[g // GH] + g % GH // 2
                nc.vector.tensor_tensor(h[:, g, :], ps[0:S, bank, g % 2 * D:g % 2 * D + D], h[:, g, :],
                                        ALU.add).then_inc(added, 1)

            def col(half, stage, n):
                return acol[:, half, stage, n, :]

            def softmax_shift(stage, half):
                lg, e = blocks(L_BANK[stage][half]), att[half]["e"]
                dve.wait_ge(att_logits[stage], half + 1)
                nc.vector.tensor_reduce(col(half, stage, 0).rearrange("p (b s) -> p b s", b=2), lg, AX.X,
                                        ALU.max).then_inc(att_max[stage], 1)
                dve.wait_ge(att_max[stage], half + 1)
                if stage == 1:
                    dve.wait_ge(att_weighted[0], half + 1)
                nc.vector.tensor_tensor(halves(e[:]), lg, spread(col(half, stage, 0)), ALU.subtract)\
                    .then_inc(att_shift[stage], 1)

            def softmax_mean(stage, half):
                e = att[half]["e"]
                dve.wait_ge(att_exp[stage], half + 1)
                nc.vector.tensor_reduce(col(half, stage, 1), e[:], AX.X, ALU.add).then_inc(att_sum[stage], 1)
                dve.wait_ge(att_weighted[stage], half + 1)
                nc.vector.tensor_reduce(col(half, stage, 2), att[half]["w"][:], AX.X, ALU.add).then_inc(att_wsum[stage], 1)
                dve.wait_ge(att_sum[stage], half + 1)
                nc.vector.reciprocal(col(half, stage, 3), col(half, stage, 1)).then_inc(att_rsum[stage], 1)
                dve.wait_ge(att_wsum[stage], half + 1)
                dve.wait_ge(att_rsum[stage], half + 1)
                nc.vector.tensor_tensor(col(half, stage, 4), col(half, stage, 2), col(half, stage, 3), ALU.mult)\
                    .then_inc(att_glob[stage], 1)
                dve.wait_ge(att_glob[stage], half + 1)
                src, done = (("k", kq_ready), ("v", u_ready))[stage]
                dve.wait_ge(proj_held[src], half + 1)
                nc.vector.tensor_tensor(halves(att[half]["w"][:]), halves(att[half][src][:]),
                                        spread(col(half, stage, 4)), ALU.mult).then_inc(done, 1)

            steps = [0]

            def step(ins):
                steps[0] += 1
                ins.then_inc(route_step, 1)
                dve.wait_ge(route_step, steps[0])

            def per_group(c):
                return c.unsqueeze(2).broadcast_to([S, GH, E])

            def route_shifts(half):
                gs = slice(GH * half, GH * half + GH)
                lg = ps[0:S, OUT_BANK[half], 0:GH * E].rearrange("p (g e) -> p g e", g=GH)
                dve.wait_ge(router_ready, half + 1)
                step(nc.vector.tensor_reduce(cols[:, half, 0, :], lg, AX.X, ALU.max))
                nc.vector.tensor_tensor(shifted[:, gs, :], lg, per_group(cols[:, half, 0, :]), ALU.subtract)\
                    .then_inc(route_shift, 1)

            def flat(t):
                return t.rearrange("p g e -> p (g e)")

            def route_choose(half):
                gs = slice(GH * half, GH * half + GH)
                rank = const("rank", S)
                rank3 = rank.rearrange("p (g e) -> p g e", g=GH)
                first, second = (chosen[:, half, c, :].rearrange("p (g e) -> p g e", g=GH) for c in range(2))
                dve.wait_ge(route_exp, half + 1)
                step(nc.vector.scalar_tensor_tensor(flat(ranked[:, gs, :]), flat(ex[:, gs, :]), 1.0, rank, ALU.is_ge, ALU.mult))
                step(nc.vector.tensor_reduce(cols[:, half, 3, :], ranked[:, gs, :], AX.X, ALU.max))
                nc.vector.tensor_tensor(first, rank3, per_group(cols[:, half, 3, :]), ALU.is_equal).then_inc(first_ready, 1)
                nc.vector.tensor_reduce(cols[:, half, 1, :], ex[:, gs, :], AX.X, ALU.add)
                dve.wait_ge(first_ready, half + 1)
                step(nc.vector.scalar_tensor_tensor(flat(ex2[:, gs, :]), chosen[:, half, 0, :], -2.0, flat(ex[:, gs, :]),
                                                    ALU.mult, ALU.add))
                step(nc.vector.tensor_reduce(cols[:, half, 4, :], ex2[:, gs, :], AX.X, ALU.max))
                step(nc.vector.tensor_tensor(ranked2[:, gs, :], ex2[:, gs, :], per_group(cols[:, half, 4, :]), ALU.is_equal))
                step(nc.vector.tensor_tensor(ranked[:, gs, :], ranked2[:, gs, :], rank3, ALU.mult))
                step(nc.vector.tensor_reduce(cols[:, half, 5, :], ranked[:, gs, :], AX.X, ALU.max))
                nc.vector.tensor_tensor(second, rank3, per_group(cols[:, half, 5, :]), ALU.is_equal).then_inc(choice_ready, 1)
                nc.vector.reciprocal(cols[:, half, 2, :], cols[:, half, 1, :]).then_inc(rsum_ready, 1)

            def route_slots(half):
                dve.wait_ge(choice_ready, half + 1)
                dve.wait_ge(cum_ready, half + 1)
                cum = ps[0:S, OUT_BANK[half] + 1, 0:2 * GH * E]
                nc.vector.tensor_tensor(slot2[:, half].rearrange("p c n -> p (c n)"), chosen[:, half].rearrange("p c n -> p (c n)"),
                                        cum, ALU.mult).then_inc(cum_used, 1)
                dve.wait_ge(cum_used, half + 1)
                nc.vector.tensor_tensor(slot[:, half, :], slot2[:, half, 0, :], slot2[:, half, 1, :], ALU.add).then_inc(slot_ready, 1)
                dve.wait_ge(slot_ready, half + 1)
                for p in range(2):
                    g0 = GH * half + 2 * p
                    n = 2 * E
                    nc.vector.tensor_tensor(
                        disp[:, g0:g0 + 2, :].rearrange("p g (e c) -> p (g e) c", e=E),
                        slot[:, half, p * n:p * n + n].unsqueeze(2).broadcast_to([S, n, CAP]),
                        const("iota", S).unsqueeze(1).broadcast_to([S, n, CAP]), ALU.is_equal).then_inc(disp_ready, 1)

            def slots_lo(g):
                bank = DISP_BANK[g % 2]
                for c in range(2):
                    dve.wait_ge(ei_hi_ready, 2 * g + c + 1)
                    sl = (slice(None), slice(None), slice(g * CAP, g * CAP + CAP))
                    src = ps[:, bank + c, 0:EC].rearrange("p (e c) -> p e c", e=E)
                    nc.vector.tensor_tensor(ei["ab"[c], "lo"][sl], src, ei["ab"[c], "hi"][sl].bitcast(F32),
                                            ALU.subtract).then_inc(ei_lo_ready, 1)

            def hidden_lo(e):
                for pair in range(FT // 2):
                    dve.wait_ge(hid_hi, 3 * e + pair + 1)
                    if e >= 2 and pair == 0:
                        dve.wait_ge(y_psum, e - 1)
                    nc.vector.scalar_tensor_tensor(
                        h_lo[e % 2][:, 2 * pair:2 * pair + 2, :].rearrange("p t s -> p (t s)"),
                        ps[:, 3 * (e % 2) + pair, 0:2 * SLOTS], 0.0,
                        h_hi[e % 2][:, 2 * pair:2 * pair + 2, :].rearrange("p t s -> p (t s)").bitcast(F32),
                        ALU.max, ALU.subtract).then_inc(hid_lo, 1)

            def hold_y(e):
                dve.wait_ge(y_psum, e + 1)
                if e >= 2:
                    dve.wait_ge(y_moved[e % 2], 16 * 8 * (e // 2))
                nc.vector.tensor_copy(y[:, e % 2].rearrange("p h d -> p (h d)"), ps[0:HS, 6 + e % 2, 0:2 * D]).then_inc(y_held, 1)

            nc.vector.memset(xnt_b[DB:DB + 1, :], 1.0).then_inc(ones_row, 1)
            dve.wait_ge(small_loaded, 16)
            at = SMALL["wqk"][0]
            for j in range(4):
                nc.vector.tensor_scalar(blk[:, j, :], const("mask"), small[:, at + j:at + j + 1], SCALE, ALU.mult,
                                        ALU.mult).then_inc(blk_ready, 1)
            nc.vector.tensor_copy(tri[:], const("tri", S)).then_inc(cast_ready, 1)
            nc.vector.tensor_copy(ones[:], const("ones", S)).then_inc(cast_ready, 1)
            for p in range(4):
                norm_pair(p, embedded)
            softmax_shift(0, 0)
            softmax_mean(0, 0)
            softmax_shift(0, 1)
            softmax_shift(1, 0)
            softmax_mean(0, 1)
            softmax_mean(1, 0)
            softmax_shift(1, 1)
            norm_pair(4, attended)
            norm_pair(5, attended)
            softmax_mean(1, 1)
            route_shifts(0)
            route_choose(0)
            route_slots(0)
            norm_pair(6, attended)
            norm_pair(7, attended)
            for g in range(4):
                slots_lo(g)
            route_shifts(1)
            route_choose(1)
            route_slots(1)
            for g in range(4, 8):
                slots_lo(g)
            hidden_lo(0)
            for e in range(E):
                if e + 1 < E:
                    hidden_lo(e + 1)
                hold_y(e)
            for p in range(4):
                dve.wait_ge(mix_psum, p + 1)
                for i in range(2):
                    g = 2 * p + i
                    nc.vector.tensor_tensor(res[:, g, :], ps[0:S, p, i * 256:i * 256 + D], h[:, g, :], ALU.add).then_inc(res_ready, 1)

        @block.gpsimd
        def _(pool):
            def inverse_std(p):
                gs = slice(2 * (p % GH), 2 * (p % GH) + 2)
                pool.wait_ge(ln_moments, 2 * p + 2)
                nc.gpsimd.tensor_tensor(var[:, gs], moments[:, gs, 1], const("eps", S), ALU.add).then_inc(ln_var, 1)
                pool.wait_ge(ln_var, p + 1)
                nc.gpsimd.tensor_tensor(rstd[:, gs], var[:, gs], const("power", S), ALU.pow).then_inc(ln_rstd, 1)

            def weigh(stage, half):
                pool.wait_ge(att_exp[stage], half + 1)
                src = "qk"[stage]
                pool.wait_ge(proj_held[src], half + 1)
                if stage == 1:
                    pool.wait_ge(att_logits[1], half + 1)
                nc.gpsimd.tensor_tensor(att[half]["w"][:], att[half]["e"][:], att[half][src][:], ALU.mult)\
                    .then_inc(att_weighted[stage], 1)

            def split_in(e):
                pool.wait_ge(wi_hi, e + 1)
                nc.gpsimd.tensor_tensor(w_lo[e % 2][:, 0:WI_W], raw[:, e % 2, 0:WI_W],
                                        w_hi[e % 2][:, 0:WI_W].bitcast(F32), ALU.subtract).then_inc(wi_lo, 1)

            def split_out(e):
                pool.wait_ge(wo_hi, e + 1)
                nc.gpsimd.tensor_tensor(w_lo[e % 2][:, WO:WEXP], raw[:, e % 2, WO:WEXP],
                                        w_hi[e % 2][:, WO:WEXP].bitcast(F32), ALU.subtract).then_inc(wo_lo, 1)

            def split_x(half):
                pool.wait_ge(x_hi_ready, half + 1)
                gs = slice(GH * half, GH * half + GH)
                nc.gpsimd.tensor_tensor(x_lo[:, gs, 0:DA], xn[:, gs, 0:DA], x_hi[:, gs, 0:DA].bitcast(F32), ALU.subtract)
                for c in (DA, DA + DB):
                    last = nc.gpsimd.tensor_tensor(x_lo[:, gs, c:c + DB], xn[:, gs, DA:D],
                                                   x_hi[:, gs, c:c + DB].bitcast(F32), ALU.subtract)
                last.then_inc(x_lo_ready, 1)

            def gates(half):
                gs = slice(GH * half, GH * half + GH)
                n = GH * E
                pool.wait_ge(rsum_ready, half + 1)
                pool.wait_ge(choice_ready, half + 1)
                nc.gpsimd.tensor_tensor(gate[:, half, 0, :], chosen[:, half, 0, :], chosen[:, half, 1, :], ALU.add)\
                    .then_inc(gate_step, 1)
                nc.gpsimd.tensor_tensor(gate[:, half, 1, :].rearrange("p (g e) -> p g e", g=GH), ex[:, gs, :],
                                        cols[:, half, 2, :].unsqueeze(2).broadcast_to([S, GH, E]), ALU.mult)\
                    .then_inc(gate_step, 1)
                pool.wait_ge(gate_step, 3 * half + 2)
                nc.gpsimd.tensor_tensor(gate[:, half, 2, :], gate[:, half, 0, :], gate[:, half, 1, :], ALU.mult)\
                    .then_inc(gate_step, 1)
                pool.wait_ge(gate_step, 3 * half + 3)
                pool.wait_ge(disp_ready, 2 * half + 2)
                nc.gpsimd.tensor_tensor(comb[:, gs, :].rearrange("p g (e c) -> p (g e) c", e=E),
                                        disp[:, gs, :].rearrange("p g (e c) -> p (g e) c", e=E).bitcast(F32),
                                        gate[:, half, 2, :].unsqueeze(2).broadcast_to([S, n, CAP]), ALU.mult)\
                    .then_inc(comb_ready, 1)

            pool.wait_ge(small_loaded, 16)
            for p in range(4):
                inverse_std(p)
            weigh(0, 0)
            weigh(0, 1)
            weigh(1, 0)
            split_in(0)
            inverse_std(4)
            inverse_std(5)
            weigh(1, 1)
            split_x(0)
            inverse_std(6)
            inverse_std(7)
            gates(0)
            split_out(0)
            split_x(1)
            gates(1)
            split_in(1)
            for e in range(E - 1):
                if e + 2 < E:
                    split_in(e + 2)
                split_out(e + 1)


def kernel(**inputs):
    import concourse.bacc as _bacc
    from concourse.bass_utils import run_bass_kernel_spmd as _run

    a = {k: np.asarray(v) for k, v in inputs.items()}
    f32 = np.float32

    xi = a["x"].reshape(IMAGES, 3, 7, 16, 7, 16).transpose(3, 5, 1, 0, 2, 4).reshape(KT, 128, 4, 2 * S)
    xi = np.ascontiguousarray(xi.transpose(2, 1, 0, 3)).reshape(4, 128, KT * 2 * S)
    wt = np.ascontiguousarray(a["L0_tok_W_lin"].T.reshape(KT, 128, D).transpose(1, 0, 2)).reshape(128, KT * D)

    wq = a["L0_attn_Wqkv"].T
    wqkv = np.zeros((128, 2, QKV_W), f32)
    for k, rows in enumerate((slice(0, DA), slice(DA, D))):
        n = rows.stop - rows.start
        wqkv[:n, k, 0:D] = wq[rows, 0:D]
        for j in range(3):
            at = D + QKV_J * j
            wqkv[:n, k, at:at + DA] = wq[rows, D * j:D * j + DA]
            wqkv[:n, k, at + DA + DB:at + DA + 2 * DB] = wq[rows, D * j + DA:D * j + D]
    wqkv[DB, 1, 0:D] = a["L0_attn_bp"]

    small = np.zeros((128, SMALL_W), f32)

    def put(name, value):
        at, w = SMALL[name]
        value = np.asarray(value)
        small[:value.shape[0], at:at + w] = value

    put("bias", np.broadcast_to(a["L0_tok_b_lin"], (128, D)))
    head = np.arange(128) // HD
    put("mask", (head[:, None] == head[None, :]).astype(f32))
    wqv, wkv = a["L0_attn_w_q"].reshape(D), a["L0_attn_w_k"].reshape(D)
    put("wqk", np.stack([wqv[:DA], np.tile(wqv[DA:], 2), wkv[:DA], np.tile(wkv[DA:], 2)], axis=1))
    put("ident", np.eye(128, dtype=f32))
    wp = a["L0_attn_Wp"].T
    put("wp_a", wp[:DA])
    put("wp_b", np.concatenate([wp[DA:], wp[DA:]]))
    put("router_a", a["L0_ffn_w_router"][:DA])
    put("router_b", a["L0_ffn_w_router"][DA:])
    put("tri", np.triu(np.ones((S, S), f32)))
    put("ones", np.ones((S, S), f32))
    put("rank", np.broadcast_to(np.tile(E - np.arange(E, dtype=f32), GH), (S, GH * E)))
    put("iota", np.broadcast_to(np.arange(1, CAP + 1, dtype=f32), (S, CAP)))

    put("eps", np.full((S, 2), EPS, f32))
    put("power", np.full((S, 2), -0.5, f32))

    wi, wo = a["L0_ffn_wi"], a["L0_ffn_wo"]
    wexp = np.empty((E, 128, WEXP), f32)
    wexp[:, :, 0:F] = wi[:, :DA]
    wexp[:, :DB, WI_B:WO] = wi[:, DA:, 0:F // 2]
    wexp[:, DB:, WI_B:WO] = wi[:, DA:, F // 2:]
    wexp[:, :, WO:] = wo.reshape(E, FT, 128, D).transpose(0, 2, 1, 3).reshape(E, 128, FT * D)

    arrays = {"x_dram": xi, "wtok_dram": wt, "wqkv_dram": wqkv.reshape(128, 2 * QKV_W), "small_dram": small,
              "wexp_dram": wexp}
    nc = _bacc.Bacc("TRN2", target_bir_lowering=False, num_devices=1)
    args = [nc.dram_tensor(k, v.shape, F32, kind="ExternalInput").ap() for k, v in arrays.items()]
    out = nc.dram_tensor("out_0_dram", (IMAGES * N_TOK, D), F32, kind="ExternalOutput").ap()
    build(nc, *args, out)
    r = _run(nc, [arrays], core_ids=[0])
    return r.results[0]["out_0_dram"].reshape(IMAGES, N_TOK, D)
```

```python
from contextlib import ExitStack

import numpy as np

import concourse.bass as bass
from concourse import mybir

F32 = mybir.dt.float32
F32R = mybir.dt.float32r
BF16 = mybir.dt.bfloat16
ALU = mybir.AluOpType
ACT = mybir.ActivationFunctionType
AX = mybir.AxisListType

IMAGES, N_TOK, D = 16, 49, 192
PATCH = 768
KT = PATCH // 128
HEADS, HD = 12, 16
SCALE = float(HD) ** -0.5
EPS = 1e-5
E, F, CAP = 8, 768, 30
G, S = 8, 98
GH = G // 2
TH = GH * S
DA, DB = 128, 64
FT = F // 128
HS = GH * CAP
SLOTS = G * CAP
EC = E * CAP

NB = 12
B_COLS = 4 * N_TOK
A_COLS = 2 * B_COLS

QKV_J = DA + DB + DB + DB
QKV_W = 3 * QKV_J
SMALL = {}


def _place(name, width, at=[0]):
    SMALL[name] = (at[0], width)
    at[0] += width


_place("bias", D)
_place("ident", 128)
_place("eps", 2)
_place("power", 2)
_place("mask", 128)
_place("wqk", 4)
SMALL_FIRST = SMALL["wqk"][0] + SMALL["wqk"][1]
_place("bp", D)
_place("wp_a", D)
_place("wp_b", D)
_place("router_a", E)
_place("router_b", E)
_place("tri", S)
_place("ones", S)
_place("rank", GH * E)
_place("iota", CAP)
SMALL_W = sum(w for _, w in SMALL.values())

WO = F
WEXP = WO + FT * D


def build(nc, x_in, wtok_in, wqkv_in, small_in, wexp_in, wexp_b_in, out):
    ctx = ExitStack()
    with ctx:
        def sb(name, shape, dt=F32, scope=ctx):
            return scope.enter_context(nc.sbuf_tensor(name, shape, dt))

        def sem(name):
            return ctx.enter_context(nc.semaphore(name))

        ps = ctx.enter_context(nc.psum_tensor("ps", [128, 8, 512], F32))

        small = sb("small", [128, SMALL_W])

        def const(name, rows=128):
            at, w = SMALL[name]
            return small[0:rows, at:at + w]

        filler = sb("filler", [128, 512], BF16)
        tri = sb("tri", [S, S], BF16)
        ones = sb("ones", [S, S], BF16)
        blk = sb("blk", [128, 4, 128])
        h = sb("h", [S, G, D])
        xn = sb("xn", [S, G, D])
        stats = sb("stats", [S, G, 6])
        moments = sb("moments", [S, G, 2])
        var = sb("var", [S, G])
        rstd = sb("rstd", [S, G])
        xn2t_a = sb("xn2t_a", [128, G, S])
        xn2t_b = sb("xn2t_b", [DB, G, S])
        x_lo = sb("x_lo", [S, G, D + DB], F32R)
        shifted = sb("shifted", [S, G, E])
        ex = sb("ex", [S, G, E])
        ex2 = sb("ex2", [S, G, E])
        ranked = sb("ranked", [S, G, E])
        ranked2 = sb("ranked2", [S, G, E])
        chosen = sb("chosen", [S, 2, 2, GH * E], BF16)
        slot2 = sb("slot2", [S, 2, 2, GH * E])
        slot = sb("slot", [S, 2, GH * E])
        gate = sb("gate", [S, 2, 3, GH * E])
        cols = sb("cols", [S, 2, 6, GH])
        disp = sb("disp", [S, G, EC], F32R)
        comb = sb("comb", [S, G, EC])
        comb7 = sb("comb7", [S, G, HS])
        ei = [sb(f"ei_{p}", [128, 2, E, SLOTS], F32R) for p in ("hi", "lo")]
        raw = sb("raw", [128, 2, WEXP])
        raw_b = sb("raw_b", [DB, 2, F])
        w = [sb(f"wexp{i}", [128, 2, WEXP], F32R) for i in range(2)]
        w_b = [sb(f"wexp_b{i}", [128, F], F32R) for i in range(2)]

        early = ExitStack()
        wqkv_hi = sb("wqkv_hi", [128, 2, QKV_W], F32R, early)
        wqkv_lo = sb("wqkv_lo", [128, 2, QKV_W], F32R, early)
        xnt_a = [sb(f"xnt_a_{p}", [128, G * S], F32R, early) for p in ("hi", "lo")]
        xnt_b = sb("xnt_b", [128, G * S], F32R, early)
        acol = sb("acol", [128, 2, 2, 5, NB], F32, early)

        def attention_tensors(half, names):
            return {n: sb(f"{n}{half}", [128, NB, N_TOK], F32, early) for n in names}

        att = [attention_tensors(0, "q"), attention_tensors(1, "")]
        unsplit = ExitStack()
        wqkv = sb("wqkv", [128, 2, QKV_W], F32, unsplit)
        unsplit.close()
        att[0].update(attention_tensors(0, "kvew"))
        embedding = ExitStack()
        x = sb("x", [128, 4, KT, 2 * S], F32, embedding)
        wtok = sb("wtok", [128, KT, D], F32, embedding)
        embedding.close()
        att[1].update(attention_tensors(1, "qkvew"))
        x_hi = sb("x_hi", [S, G, D + DB], F32R, early)
        early.close()
        h_hi = [sb(f"h_hi{i}", [128, FT, SLOTS], F32R) for i in range(2)]
        h_lo = [sb(f"h_lo{i}", [128, FT, SLOTS], F32R) for i in range(2)]
        y = sb("y", [HS, 2, 2, D])
        y_all = sb("y_all", [HS, 2, G, D])
        res = sb("res", [S, G, D])
        combT = sb("combT", [HS, G, 2, S])
        comb7T = sb("comb7T", [HS, G, S])
        y_low = sb("y_low", [HS, 2, D])

        x_loaded = [sem(f"x_loaded{c}") for c in range(5)]
        wtok_loaded = [sem(f"wtok_loaded{c}") for c in range(2)]
        filler_ready = sem("filler_ready")
        small_loaded = sem("small_loaded")
        wqkv_loaded = sem("wqkv_loaded")
        tables_loaded = sem("tables_loaded")
        qkv_hi = sem("qkv_hi")
        qkv_lo = sem("qkv_lo")
        biased = sem("biased")
        cast_ready = sem("cast_ready")
        blk_ready = sem("blk_ready")
        tok_ready = sem("tok_ready")
        added = sem("added")
        ln_stats = sem("ln_stats")
        ln_moments = sem("ln_moments")
        ln_var = sem("ln_var")
        ln_rstd = sem("ln_rstd")
        xn_ready = sem("xn_ready")
        tr_ready = sem("tr_ready")
        xnt_hi_ready = sem("xnt_hi_ready")
        xnt_lo_ready = sem("xnt_lo_ready")
        proj_ready = {j: sem(f"{j}_ready") for j in "qkv"}
        proj_held = {j: sem(f"{j}_held") for j in "qkv"}
        att_logits = [sem(f"att_logits{a}") for a in (1, 2)]
        att_max = [sem(f"att_max{a}") for a in (1, 2)]
        att_shift = [sem(f"att_shift{a}") for a in (1, 2)]
        att_exp = [sem(f"att_exp{a}") for a in (1, 2)]
        att_sum = [sem(f"att_sum{a}") for a in (1, 2)]
        att_weighted = [sem(f"att_weighted{a}") for a in (1, 2)]
        att_wsum = [sem(f"att_wsum{a}") for a in (1, 2)]
        att_rsum = [sem(f"att_rsum{a}") for a in (1, 2)]
        att_glob = [sem(f"att_glob{a}") for a in (1, 2)]
        kq_ready = sem("kq_ready")
        u_ready = sem("u_ready")
        attn_out = sem("attn_out")
        tr2_ready = sem("tr2_ready")
        xn2t_ready = sem("xn2t_ready")
        router_ready = sem("router_ready")
        x_hi_ready = sem("x_hi_ready")
        x_lo_ready = sem("x_lo_ready")
        route_step = sem("route_step")
        route_exp = sem("route_exp")
        route_shift = sem("route_shift")
        first_ready = sem("first_ready")
        choice_ready = sem("choice_ready")
        cum_ready = sem("cum_ready")
        cum_used = sem("cum_used")
        slot_ready = sem("slot_ready")
        disp_ready = sem("disp_ready")
        rsum_ready = sem("rsum_ready")
        gate_step = sem("gate_step")
        comb_ready = sem("comb_ready")
        ei_psum = sem("ei_psum")
        ei_hi_ready = sem("ei_hi_ready")
        ei_lo_ready = sem("ei_lo_ready")
        combT_psum = sem("combT_psum")
        combT_ready = sem("combT_ready")
        comb7_zero = sem("comb7_zero")
        comb7_ready = sem("comb7_ready")
        comb7T_psum = sem("comb7T_psum")
        comb7T_ready = sem("comb7T_ready")
        y_low_held = sem("y_low_held")
        wi_loaded = [sem(f"wi_loaded{i}") for i in range(2)]
        wo_loaded = [sem(f"wo_loaded{i}") for i in range(2)]
        wi_hi = sem("wi_hi")
        wi_lo = sem("wi_lo")
        wi_b_lo = sem("wi_b_lo")
        wo_hi = sem("wo_hi")
        wo_lo = sem("wo_lo")
        hid_psum = sem("hid_psum")
        hid_hi = sem("hid_hi")
        hid_lo = sem("hid_lo")
        y_psum = sem("y_psum")
        y_held = sem("y_held")
        y_moved = [sem(f"y_moved{i}") for i in range(2)]
        mix_psum = sem("mix_psum")
        res_ready = sem("res_ready")
        stored = sem("stored")

        block = ctx.enter_context(nc.Block())

        def blocks(bank):
            quads = ps[:, bank:bank + 2, :].rearrange("p b (h c) -> p (b h) c", h=2)[:, 0:NB // 4, 0:B_COLS]
            return quads.rearrange("p b (s n) -> p b s n", n=N_TOK)

        def a_blocks(bank):
            return ps[:, bank, :].rearrange("p (h c) -> p h c", h=2)[:, :, 0:B_COLS]

        def quads(t):
            return t.rearrange("p (b s) n -> p b s n", b=NB // 4)

        def spread(col):
            return col.rearrange("p (b s) -> p b s", b=NB // 4).unsqueeze(3).broadcast_to([128, NB // 4, 4, N_TOK])

        EMBED_BANK = 0
        TURN_BANK = 2
        PROJ_BANK = {"q": (4, 0), "k": (6, 6), "v": (4, 0)}
        LOGIT_BANK = ((2, 2), (6, 6))
        OUT_BANK = (4, 0)
        DISP_BANK = 4
        COMBT_BANK = (2, 6)
        COMB7T_BANK = 3
        FILL_BANK = 7

        def dispatched(g):
            return ps[:, DISP_BANK + g % 2, 0:2 * EC].rearrange("p (k e c) -> p k e c", k=2, e=E)

        def slots_of(t, g):
            return t[:, :, :, g * CAP:g * CAP + CAP]

        @block.sync
        def _(sp):
            half_k = KT // 2
            wtok_v = wtok_in.rearrange("p (k d) -> p k d", k=KT)
            x_v = x_in.rearrange("c p (k t) -> c p k t", k=KT)
            for k in (0, half_k):
                sp.dma_start(wtok[:, k:k + half_k, :], wtok_v[:, k:k + half_k, :]).then_inc(wtok_loaded[k // half_k], 16)
                sp.dma_start(x[:, 0, k:k + half_k], x_v[0, :, k:k + half_k]).then_inc(x_loaded[k // half_k], 16)
            sp.dma_start(small[:, 0:SMALL_FIRST], small_in[:, 0:SMALL_FIRST]).then_inc(small_loaded, 16)
            sp.dma_start(x[:, 1], x_v[1]).then_inc(x_loaded[2], 16)
            sp.dma_start(wqkv[:].rearrange("p k d -> p (k d)"), wqkv_in).then_inc(wqkv_loaded, 16)
            sp.dma_start(small[:, SMALL_FIRST:], small_in[:, SMALL_FIRST:]).then_inc(tables_loaded, 16)
            sp.dma_start(x[:, 2], x_v[2]).then_inc(x_loaded[3], 16)
            sp.dma_start(x[:, 3], x_v[3]).then_inc(x_loaded[4], 16)

            def load_in(e):
                sp.dma_start(raw[:, e % 2, 0:WO], wexp_in[e, :, 0:WO]).then_inc(wi_loaded[e % 2], 16)
                sp.dma_start(raw_b[:, e % 2, :], wexp_b_in[e]).then_inc(wi_loaded[e % 2], 16)

            def load_out(e):
                sp.dma_start(raw[:, e % 2, WO:WEXP], wexp_in[e, :, WO:WEXP]).then_inc(wo_loaded[e % 2], 16)

            def move_y(e):
                sp.wait_ge(y_held, e + 1)
                dst = y_all[CAP * (e % 4):CAP * (e % 4) + CAP, e // 4].rearrange("c (h g) d -> c h g d", h=2)
                for g in range(GH):
                    sp.dma_start(dst[:, :, g, :], y[g * CAP:g * CAP + CAP, e % 2]).then_inc(y_moved[e % 2], 16)

            for e in range(2):
                load_in(e)
                load_out(e)
            for e in range(2, E):
                sp.wait_ge(wi_hi, e - 1)
                sp.wait_ge(wi_lo, e - 1)
                sp.wait_ge(wi_b_lo, e - 1)
                load_in(e)
                sp.wait_ge(wo_hi, e - 1)
                sp.wait_ge(wo_lo, e - 1)
                load_out(e)
                if e >= 3:
                    move_y(e - 3)
            for e in range(E - 3, E - 1):
                move_y(e)
            for g in range(G):
                sp.wait_ge(res_ready, g + 1)
                sp.dma_start(out[g * S:(g + 1) * S, :], res[:, g, :]).then_inc(stored, 16)
            sp.wait_ge(stored, 16 * G)

        @block.tensor
        def _(pe):
            def mm(o, a, b, first, last):
                return nc.tensor.matmul(o, a, b, start=first, stop=last)

            def mm3(o, a, b, first, last):
                mm(o, a[0], b[0], first, False)
                mm(o, a[0], b[1], False, False)
                return mm(o, a[1], b[0], False, last)

            def embed(g):
                if g > 0 and g % 2 == 0:
                    pe.wait_ge(x_loaded[g // 2 + 1], 16)
                if g >= 2:
                    pe.wait_ge(added, g - 1)
                for k in range(KT):
                    if g == 0 and k % (KT // 2) == 0:
                        pe.wait_ge(wtok_loaded[k // (KT // 2)], 16)
                        pe.wait_ge(x_loaded[k // (KT // 2)], 16)
                    last = mm(ps[0:S, EMBED_BANK + g % 2, 0:D], x[:, g // 2, k, (g % 2) * S:(g % 2) * S + S],
                              wtok[:, k, :], k == 0, k == KT - 1)
                last.then_inc(tok_ready, 1)

            def transposed(g, done):
                b = TURN_BANK + g % 2
                nc.tensor.transpose(ps[0:DA, b, 0:S], xn[:, g, 0:DA], const("ident", S)[:, 0:S])
                nc.tensor.transpose(ps[0:DB, b, 128:128 + S], xn[:, g, DA:D], const("ident", S)[:, 0:S]).then_inc(done, 1)

            def turn(g):
                pe.wait_ge(xn_ready, g + 1)
                if g in (4, 5):
                    pe.wait_ge(att_shift[0], 1)
                elif g >= 2:
                    pe.wait_ge(xnt_lo_ready, g - 1)
                transposed(g, tr_ready)

            def project(j, half):
                bank = PROJ_BANK[j][half]
                pe.wait_ge(xnt_lo_ready, GH * (half + 1))
                if (j, half) == ("q", 1):
                    pe.wait_ge(added, G)
                elif (j, half) == ("k", 1):
                    pe.wait_ge(att_shift[1], 1)
                elif j == "v":
                    pe.wait_ge(proj_held["q"], half + 1)
                n = "qkv".index(j)
                if half == 0:
                    pe.wait_ge(qkv_lo, 1 if j == "q" else 3)
                w0 = QKV_J * n
                t0 = TH * half

                def product(o, at, tokens, first, last):
                    hi, lo = (t[:, :, w0 + at:w0 + at + 128] for t in (wqkv_hi, wqkv_lo))
                    x_a, x_b = [t[:, tokens] for t in xnt_a], xnt_b[:, tokens]
                    mm3(o, (hi[:, 0, :], lo[:, 0, :]), x_a, first, False)
                    mm(o, hi[:, 1, :], x_b, False, False)
                    return mm(o, lo[:, 1, :], x_b, False, last)

                product(a_blocks(bank), 0, slice(t0, t0 + A_COLS), True, True)
                o = ps[:, bank + 1, 0:B_COLS]
                product(o, DA + DB, slice(t0, t0 + B_COLS), True, False)
                product(o, DA, slice(t0 + B_COLS, t0 + A_COLS), False, True).then_inc(proj_ready[j], 1)

            def logits(stage, half):
                bank = LOGIT_BANK[stage][half]
                if stage == 0:
                    pe.wait_ge(blk_ready, 4)
                    pe.wait_ge(xnt_lo_ready, GH * (half + 1))
                    pe.wait_ge(proj_held["q"], half + 1)
                    src = att[half]["q"]
                else:
                    pe.wait_ge(proj_held["k"], half + 1)
                    pe.wait_ge(kq_ready, half + 1)
                    src = att[half]["w"]
                src = src[:].rearrange("p s n -> p (s n)")
                mm(a_blocks(bank), blk[:, 2 * stage, :], src[:, 0:A_COLS], True, True)
                mm(ps[:, bank + 1, 0:B_COLS], blk[:, 2 * stage + 1, :], src[:, A_COLS:], True,
                   True).then_inc(att_logits[stage], 1)

            def fill(n):
                for _ in range(n):
                    mm(ps[:, FILL_BANK, :], filler[:, 0:128], filler[:], True, True)

            def acc(o, a, b, first, last):
                return nc.tensor.matmul(o, a, b, start=first, stop=last, skip_group_check=True)

            def out_operands(t, g):
                t = t[:].rearrange("p s n -> p (s n)")
                r, c = DB * (g // 2), A_COLS + g % 2 * S
                return t[:, g * S:g * S + S], t[r:r + DB, c:c + S], r

            def residual_q(half):
                bank = OUT_BANK[half]
                pe.wait_ge(proj_held["v"], half + 1)
                for g in range(GH):
                    q_a, q_b, r = out_operands(att[half]["q"], g)
                    o = ps[0:S, bank + g // 2, g % 2 * D:g % 2 * D + D]
                    acc(o[:, 0:DA], q_a, const("ident"), g % 2 == 0, False)
                    acc(o[:, DA:D], q_b, const("ident")[r:r + DB, r:r + DB], False, False)

            def attention_out(half):
                bank = OUT_BANK[half]
                pe.wait_ge(u_ready, half + 1)
                for g in range(GH):
                    o = ps[0:S, bank + g // 2, g % 2 * D:g % 2 * D + D]
                    u_a, u_b, r = out_operands(att[half]["w"], g)
                    acc(o, u_a, const("wp_a"), False, False)
                    last = acc(o, u_b, const("wp_b")[r:r + DB, :], False, g % 2 == 1)
                    if g % 2 == 1:
                        last.then_inc(attn_out, 1)

            def turn2(g):
                pe.wait_ge(xn_ready, G + g + 1)
                if g < 2:
                    pe.wait_ge(att_shift[0], 2)
                else:
                    pe.wait_ge(xn2t_ready, g - 1)
                transposed(g, tr2_ready)

            def router(half):
                bank = OUT_BANK[half]
                for g in range(GH):
                    gg = GH * half + g
                    pe.wait_ge(xn2t_ready, gg + 1)
                    o = ps[0:S, bank, g * E:g * E + E]
                    mm(o, xn2t_a[:, gg, :], const("router_a"), True, False)
                    last = mm(o, xn2t_b[:, gg, :], const("router_b", DB), False, True)
                last.then_inc(router_ready, 1)

            def cumulate(half):
                bank = OUT_BANK[half] + 1
                pe.wait_ge(first_ready, half + 1)
                mm(ps[0:S, bank, 0:GH * E], tri[:], chosen[:, half, 0, :], True, True)
                mm(ps[0:S, bank, GH * E:2 * GH * E], ones[:], chosen[:, half, 0, :], True, False)
                pe.wait_ge(choice_ready, half + 1)
                mm(ps[0:S, bank, GH * E:2 * GH * E], tri[:], chosen[:, half, 1, :], False, True).then_inc(cum_ready, 1)

            def dispatch(g):
                pe.wait_ge(x_lo_ready, g // 2 + 1)
                pe.wait_ge(disp_ready, g // 2 + 1)
                if g < 2:
                    pe.wait_ge(cum_used, 1)
                else:
                    pe.wait_ge(ei_lo_ready, g - 1)
                for c in range(2):
                    o = ps[:, DISP_BANK + g % 2, c * EC:c * EC + EC]
                    for part in (x_hi, x_lo):
                        last = mm(o, part[:, g, c * 128:c * 128 + 128], disp[:, g, :], part is x_hi, part is x_lo)
                last.then_inc(ei_psum, 1)

            def turn_comb(half):
                pe.wait_ge(comb_ready, half + 1)
                if half == 0:
                    pe.wait_ge(xn2t_ready, G)
                else:
                    pe.wait_ge(cum_used, 2)
                for q in range(4):
                    g = GH * half + q
                    b = COMBT_BANK[half] + q // 2
                    for s in range(2):
                        c = (q % 2 * 2 + s) * 128
                        rows = (HS, HS - CAP)[s]
                        last = nc.tensor.transpose(ps[0:rows, b, c:c + S], comb[:, g, s * HS:s * HS + rows],
                                                   const("ident", S)[:, 0:S])
                last.then_inc(combT_psum, 1)

            def turn_comb7():
                pe.wait_ge(comb7_ready, 2)
                for g in range(G):
                    last = nc.tensor.transpose(ps[0:HS, COMB7T_BANK + g // GH, g % GH * 128:g % GH * 128 + S],
                                               comb7[:, g, :], const("ident", S)[:, 0:S])
                last.then_inc(comb7T_psum, 1)

            def expert_in(e, pairs=range(FT // 2)):
                pe.wait_ge(wi_hi, e + 1)
                pe.wait_ge(wi_lo, e + 1)
                pe.wait_ge(wi_b_lo, e + 1)
                buf = e % 2
                for pair in pairs:
                    for t in range(2):
                        f = 2 * pair + t
                        o = ps[:, 3 * buf + pair, t * SLOTS:t * SLOTS + SLOTS]
                        mm3(o, [w[buf][:, p, f * 128:f * 128 + 128] for p in range(2)], [p[:, 0, e, :] for p in ei], True, False)
                        mm(o, w_b[buf][:, f * 128:f * 128 + 128], ei[0][:, 1, e, :], False, False)
                        last = mm(o, w_b[buf][:, f * 128:f * 128 + 128], ei[1][:, 1, e, :], False, True)
                    last.then_inc(hid_psum, 1)

            def expert_out(e, buf):
                pe.wait_ge(wo_hi, e + 1)
                pe.wait_ge(wo_lo, e + 1)
                pe.wait_ge(hid_hi, 3 * (e + 1))
                pe.wait_ge(hid_lo, 3 * (e + 1))
                for half in range(2):
                    bank = ps[0:HS, 6 + half, 0:2 * D]
                    for f in range(FT):
                        cols = slice(half * HS, half * HS + HS)
                        wo = w[buf][:, :, WO + f * D:WO + f * D + D]
                        acc(bank.rearrange("p (h d) -> p h d", h=2), h_hi[buf][:, f, cols], wo, f == 0, False)
                        last = acc(bank[:, 0:D], h_lo[buf][:, f, cols], wo[:, 0, :], False, f == FT - 1)
                last.then_inc(y_psum, 1)

            def mixed(g):
                return ps[0:S, g // 2, g % 2 * 256:g % 2 * 256 + D]

            pe.wait_ge(filler_ready, 1)
            fill(13)
            for g in range(6):
                if g == 2:
                    pe.wait_ge(small_loaded, 16)
                embed(g)
                if 2 <= g < 5:
                    turn(g - 2)
            turn(3)
            project("q", 0)
            project("k", 0)
            logits(0, 0)
            embed(6)
            embed(7)
            turn(4)
            turn(5)
            project("v", 0)
            logits(1, 0)
            residual_q(0)
            turn(6)
            turn(7)
            project("q", 1)
            project("k", 1)
            logits(0, 1)
            project("v", 1)
            pe.wait_ge(tables_loaded, 16)
            attention_out(0)
            residual_q(1)
            logits(1, 1)
            pe.wait_ge(att_shift[1], 2)
            fill(3)
            pe.wait_ge(att_exp[1], 2)
            fill(5)
            turn2(0)
            turn2(1)
            fill(2)
            attention_out(1)
            turn2(2)
            turn2(3)
            router(0)
            fill(2)
            turn2(4)
            turn2(5)
            fill(2)
            turn2(6)
            turn2(7)
            fill(2)
            router(1)
            pe.wait_ge(cast_ready, 2)
            cumulate(0)
            fill(4)
            dispatch(0)
            dispatch(1)
            fill(2)
            cumulate(1)
            fill(4)
            dispatch(2)
            dispatch(3)
            turn_comb(0)
            for g in range(4, 8):
                dispatch(g)
            pe.wait_ge(combT_ready, 1)
            pe.wait_ge(ei_hi_ready, G)
            pe.wait_ge(ei_lo_ready, G)
            expert_in(0, (0,))
            turn_comb7()
            expert_in(0, (1,))
            turn_comb(1)
            expert_in(0, (2,))
            for e in range(E - 1):
                if e == 0:
                    pe.wait_ge(comb7T_ready, 1)
                else:
                    pe.wait_ge(hid_lo, 3 * e)
                expert_in(e + 1)
                if e == 0:
                    pe.wait_ge(combT_ready, 2)
                else:
                    pe.wait_ge(y_held, e)
                expert_out(e, e % 2)
            pe.wait_ge(y_held, E - 1)
            expert_out(E - 1, (E - 1) % 2)

            pe.wait_ge(hid_lo, 3 * E)
            pe.wait_ge(y_moved[0], 16 * GH * 2)
            pe.wait_ge(y_moved[1], 16 * GH * 2)
            for g in range(G):
                acc(mixed(g), combT[:, g, 0, :], y_all[:, 0, g, :], g % 2 == 0, False)
            pe.wait_ge(y_held, E)
            for g in range(G):
                acc(mixed(g), comb7T[:, g, :], y[:, (E - 1) % 2, g // GH, :], False, False)
            pe.wait_ge(y_moved[0], 16 * GH * 4)
            pe.wait_ge(y_moved[1], 16 * GH * 3)
            n = HS - CAP
            for g in range(G):
                last = acc(mixed(g), combT[0:n, g, 1, :], y_all[0:n, 1, g, :], False, g % 2 == 1)
                if g % 2 == 1:
                    last.then_inc(mix_psum, 1)

        @block.scalar
        def _(act):
            def copy_turned(g, ready, to_a, to_b, bank, done, count):
                act.wait_ge(ready, count)
                nc.scalar.activation(to_a, ps[0:DA, bank, 0:S], ACT.Copy)
                nc.scalar.activation(to_b, ps[0:DB, bank, 128:128 + S], ACT.Copy).then_inc(done, 1)

            def hold(j, half):
                bank = PROJ_BANK[j][half]
                act.wait_ge(proj_ready[j], half + 1)
                nc.scalar.activation(quads(att[half][j][:]), blocks(bank), ACT.Copy).then_inc(proj_held[j], 1)

            def att_exps(stage, half):
                act.wait_ge(att_shift[stage], half + 1)
                e = att[half]["e"]
                nc.scalar.activation(e[:], e[:], ACT.Exp).then_inc(att_exp[stage], 1)

            def turned1(g):
                bank, cols = TURN_BANK + g % 2, slice(g * S, g * S + S)
                act.wait_ge(tr_ready, g + 1)
                nc.scalar.activation(xnt_a[0][:, cols], ps[0:DA, bank, 0:S], ACT.Copy)
                nc.scalar.activation(xnt_b[0:DB, cols], ps[0:DB, bank, 128:128 + S], ACT.Copy).then_inc(xnt_hi_ready, 1)

            def split_qkv(j):
                cols = slice(QKV_J * j, QKV_J * j + QKV_J)
                nc.scalar.activation(wqkv_hi[:, :, cols], wqkv[:, :, cols], ACT.Copy).then_inc(qkv_hi, 1)

            def turned2(g):
                copy_turned(g, tr2_ready, xn2t_a[:, g, :], xn2t_b[:, g, :], TURN_BANK + g % 2, xn2t_ready, g + 1)

            def split_x(p):
                act.wait_ge(xn_ready, G + 2 * (p + 1))
                gs = slice(2 * p, 2 * p + 2)
                nc.scalar.activation(x_hi[:, gs, 0:D], xn[:, gs, :], ACT.Copy)
                nc.scalar.activation(x_hi[:, gs, D:], xn[:, gs, DA:], ACT.Copy).then_inc(x_hi_ready, 1)

            def route_exps(half):
                act.wait_ge(route_shift, half + 1)
                gs = slice(GH * half, GH * half + GH)
                nc.scalar.activation(ex[:, gs, :], shifted[:, gs, :], ACT.Exp).then_inc(route_exp, 1)

            def slots_hi(g):
                act.wait_ge(ei_psum, g + 1)
                nc.scalar.activation(slots_of(ei[0], g), dispatched(g), ACT.Copy).then_inc(ei_hi_ready, 1)

            def split_in(e):
                act.wait_ge(wi_loaded[e % 2], 2 * 16 * (e // 2 + 1))
                if e >= 2:
                    act.wait_ge(hid_psum, 3 * (e - 1))
                nc.scalar.activation(w_b[e % 2][0:DB, :], raw_b[:, e % 2, :], ACT.Copy)
                nc.scalar.activation(w[e % 2][:, 0, 0:WO], raw[:, e % 2, 0:WO], ACT.Copy).then_inc(wi_hi, 1)

            def split_out(e):
                act.wait_ge(wo_loaded[e % 2], 16 * (e // 2 + 1))
                if e >= 2:
                    act.wait_ge(y_psum, e - 1)
                nc.scalar.activation(w[e % 2][:, 0, WO:WEXP], raw[:, e % 2, WO:WEXP], ACT.Copy).then_inc(wo_hi, 1)

            def hidden_hi(e, pairs=range(FT // 2)):
                for pair in pairs:
                    act.wait_ge(hid_psum, 3 * e + pair + 1)
                    if e >= 2 and pair == 0:
                        act.wait_ge(y_psum, e - 1)
                    nc.scalar.activation(h_hi[e % 2][:, 2 * pair:2 * pair + 2, :],
                                         ps[:, 3 * (e % 2) + pair, 0:2 * SLOTS].rearrange("p (t s) -> p t s", t=2),
                                         ACT.Relu).then_inc(hid_hi, 1)

            def turned_comb(half):
                act.wait_ge(combT_psum, half + 1)
                for s in range(2):
                    rows = (HS, HS - CAP)[s]
                    src = ps[0:rows, COMBT_BANK[half]:COMBT_BANK[half] + 2, :]
                    src = src.rearrange("p b (g e s) -> p b g e s", g=2, e=2)[:, :, :, s, 0:S]
                    dst = combT[0:rows, GH * half:GH * half + GH, s, :].rearrange("p (b g) s -> p b g s", b=2)
                    last = nc.scalar.activation(dst, src, ACT.Copy)
                last.then_inc(combT_ready, 1)

            def turned_comb7():
                act.wait_ge(comb7T_psum, 1)
                src = ps[0:HS, COMB7T_BANK:COMB7T_BANK + 2, :].rearrange("p b (g s) -> p b g s", g=GH)[:, :, :, 0:S]
                nc.scalar.activation(comb7T[:].rearrange("p (b g) s -> p b g s", b=2), src, ACT.Copy)\
                    .then_inc(comb7T_ready, 1)

            def low_y(e):
                act.wait_ge(y_psum, e + 1)
                if e >= 1:
                    act.wait_ge(y_held, e)
                nc.scalar.activation(y_low[:], ps[0:HS, 6:8, D:2 * D], ACT.Copy).then_inc(y_low_held, 1)

            act.wait_ge(wqkv_loaded, 16)
            for j in range(3):
                split_qkv(j)
            for g in range(4):
                turned1(g)
            hold("q", 0)
            hold("k", 0)
            att_exps(0, 0)
            turned1(4)
            turned1(5)
            hold("v", 0)
            split_in(0)
            att_exps(1, 0)
            turned1(6)
            turned1(7)
            split_out(0)
            hold("q", 1)
            hold("k", 1)
            att_exps(0, 1)
            hold("v", 1)
            split_in(1)
            att_exps(1, 1)
            split_x(0)
            turned2(0)
            turned2(1)
            split_x(1)
            turned2(2)
            turned2(3)
            route_exps(0)
            turned2(4)
            turned2(5)
            split_x(2)
            turned2(6)
            turned2(7)
            split_x(3)
            route_exps(1)
            slots_hi(0)
            slots_hi(1)
            slots_hi(2)
            slots_hi(3)
            turned_comb(0)
            for g in range(4, 8):
                slots_hi(g)
            hidden_hi(0, (0,))
            turned_comb7()
            hidden_hi(0, (1,))
            turned_comb(1)
            hidden_hi(0, (2,))
            for e in range(E - 1):
                if e + 2 < E:
                    split_in(e + 2)
                hidden_hi(e + 1)
                split_out(e + 1)
                low_y(e)
            low_y(E - 1)

        @block.vector
        def _(dve):
            def norm_stats(p):
                g0 = 2 * (p % GH)
                for i in range(2):
                    (embedded, attended)[p // GH](g0 + i)
                for i in range(2):
                    dve.wait_ge(added, 2 * p + i + 1)
                    nc.vector.bn_stats(stats[:, g0 + i, :], h[:, g0 + i, :]).then_inc(ln_stats, 1)
                for i in range(2):
                    dve.wait_ge(ln_stats, 2 * p + i + 1)
                    nc.vector.bn_aggr(moments[:, g0 + i, :], stats[:, g0 + i, :]).then_inc(ln_moments, 1)

            def norm_apply(p):
                dve.wait_ge(ln_rstd, p + 1)
                for i in range(2):
                    g = 2 * (p % GH) + i
                    nc.vector.tensor_scalar(xn[:, g, :], h[:, g, :], moments[:, g, 0:1], rstd[:, g:g + 1],
                                            ALU.subtract, ALU.mult).then_inc(xn_ready, 1)

            def turned1(g):
                bank, cols = TURN_BANK + g % 2, slice(g * S, g * S + S)
                dve.wait_ge(xnt_hi_ready, g + 1)
                nc.vector.tensor_tensor(xnt_a[1][:, cols], ps[0:DA, bank, 0:S], xnt_a[0][:, cols].bitcast(F32), ALU.subtract)
                nc.vector.tensor_tensor(xnt_b[DB:128, cols], ps[0:DB, bank, 128:128 + S], xnt_b[0:DB, cols].bitcast(F32),
                                        ALU.subtract).then_inc(xnt_lo_ready, 1)

            def embedded(g):
                dve.wait_ge(tok_ready, g + 1)
                nc.vector.tensor_tensor(h[:, g, :], ps[0:S, EMBED_BANK + g % 2, 0:D], const("bias", S), ALU.add).then_inc(added, 1)

            def attended(g):
                dve.wait_ge(attn_out, g // 2 + 1)
                dve.wait_ge(biased, g // 2 + 1)
                bank = OUT_BANK[g // GH] + g % GH // 2
                nc.vector.tensor_tensor(h[:, g, :], ps[0:S, bank, g % 2 * D:g % 2 * D + D], h[:, g, :],
                                        ALU.add).then_inc(added, 1)

            def col(half, stage, n):
                return acol[:, half, stage, n, :]

            def softmax_shift(stage, half):
                lg, e = blocks(LOGIT_BANK[stage][half]), att[half]["e"]
                dve.wait_ge(att_logits[stage], half + 1)
                nc.vector.tensor_reduce(col(half, stage, 0).rearrange("p (b s) -> p b s", b=NB // 4), lg, AX.X,
                                        ALU.max).then_inc(att_max[stage], 1)
                dve.wait_ge(att_max[stage], half + 1)
                if stage == 1:
                    dve.wait_ge(att_weighted[0], half + 1)
                nc.vector.tensor_tensor(quads(e[:]), lg, spread(col(half, stage, 0)), ALU.subtract)\
                    .then_inc(att_shift[stage], 1)

            def softmax_sum(stage, half):
                dve.wait_ge(att_exp[stage], half + 1)
                nc.vector.tensor_reduce(col(half, stage, 1), att[half]["e"][:], AX.X, ALU.add).then_inc(att_sum[stage], 1)
                dve.wait_ge(att_sum[stage], half + 1)
                nc.vector.reciprocal(col(half, stage, 3), col(half, stage, 1)).then_inc(att_rsum[stage], 1)

            def softmax_mean(stage, half):
                dve.wait_ge(att_weighted[stage], half + 1)
                nc.vector.tensor_reduce(col(half, stage, 2), att[half]["w"][:], AX.X, ALU.add).then_inc(att_wsum[stage], 1)
                dve.wait_ge(att_wsum[stage], half + 1)
                dve.wait_ge(att_rsum[stage], half + 1)
                nc.vector.tensor_tensor(col(half, stage, 4), col(half, stage, 2), col(half, stage, 3), ALU.mult)\
                    .then_inc(att_glob[stage], 1)
                dve.wait_ge(att_glob[stage], half + 1)
                src, done = (("k", kq_ready), ("v", u_ready))[stage]
                dve.wait_ge(proj_held[src], half + 1)
                nc.vector.tensor_tensor(quads(att[half]["w"][:]), quads(att[half][src][:]),
                                        spread(col(half, stage, 4)), ALU.mult).then_inc(done, 1)

            steps = [0]

            def step(ins):
                steps[0] += 1
                ins.then_inc(route_step, 1)
                dve.wait_ge(route_step, steps[0])

            def per_group(c):
                return c.unsqueeze(2).broadcast_to([S, GH, E])

            def route_shifts(half):
                gs = slice(GH * half, GH * half + GH)
                lg = ps[0:S, OUT_BANK[half], 0:GH * E].rearrange("p (g e) -> p g e", g=GH)
                dve.wait_ge(router_ready, half + 1)
                step(nc.vector.tensor_reduce(cols[:, half, 0, :], lg, AX.X, ALU.max))
                nc.vector.tensor_tensor(shifted[:, gs, :], lg, per_group(cols[:, half, 0, :]), ALU.subtract)\
                    .then_inc(route_shift, 1)

            def flat(t):
                return t.rearrange("p g e -> p (g e)")

            def route_first(half):
                gs = slice(GH * half, GH * half + GH)
                rank = const("rank", S)
                rank3 = rank.rearrange("p (g e) -> p g e", g=GH)
                first = chosen[:, half, 0, :].rearrange("p (g e) -> p g e", g=GH)
                dve.wait_ge(route_exp, half + 1)
                step(nc.vector.scalar_tensor_tensor(flat(ranked[:, gs, :]), flat(ex[:, gs, :]), 1.0, rank, ALU.is_ge, ALU.mult))
                step(nc.vector.tensor_reduce(cols[:, half, 3, :], ranked[:, gs, :], AX.X, ALU.max))
                nc.vector.tensor_tensor(first, rank3, per_group(cols[:, half, 3, :]), ALU.is_equal).then_inc(first_ready, 1)
                nc.vector.tensor_reduce(cols[:, half, 1, :], ex[:, gs, :], AX.X, ALU.add)

            def route_second(half):
                gs = slice(GH * half, GH * half + GH)
                rank3 = const("rank", S).rearrange("p (g e) -> p g e", g=GH)
                second = chosen[:, half, 1, :].rearrange("p (g e) -> p g e", g=GH)
                dve.wait_ge(first_ready, half + 1)
                step(nc.vector.scalar_tensor_tensor(flat(ex2[:, gs, :]), chosen[:, half, 0, :], -2.0, flat(ex[:, gs, :]),
                                                    ALU.mult, ALU.add))
                step(nc.vector.tensor_reduce(cols[:, half, 4, :], ex2[:, gs, :], AX.X, ALU.max))
                step(nc.vector.tensor_tensor(ranked2[:, gs, :], ex2[:, gs, :], per_group(cols[:, half, 4, :]), ALU.is_equal))
                step(nc.vector.tensor_tensor(ranked[:, gs, :], ranked2[:, gs, :], rank3, ALU.mult))
                step(nc.vector.tensor_reduce(cols[:, half, 5, :], ranked[:, gs, :], AX.X, ALU.max))
                nc.vector.tensor_tensor(second, rank3, per_group(cols[:, half, 5, :]), ALU.is_equal).then_inc(choice_ready, 1)
                nc.vector.reciprocal(cols[:, half, 2, :], cols[:, half, 1, :]).then_inc(rsum_ready, 1)

            def route_slots(half):
                dve.wait_ge(choice_ready, half + 1)
                dve.wait_ge(cum_ready, half + 1)
                cum = ps[0:S, OUT_BANK[half] + 1, 0:2 * GH * E]
                nc.vector.tensor_tensor(slot2[:, half].rearrange("p c n -> p (c n)"), chosen[:, half].rearrange("p c n -> p (c n)"),
                                        cum, ALU.mult).then_inc(cum_used, 1)
                dve.wait_ge(cum_used, half + 1)
                nc.vector.tensor_tensor(slot[:, half, :], slot2[:, half, 0, :], slot2[:, half, 1, :], ALU.add).then_inc(slot_ready, 1)
                dve.wait_ge(slot_ready, half + 1)
                for p in range(2):
                    g0 = GH * half + 2 * p
                    n = 2 * E
                    nc.vector.tensor_tensor(
                        disp[:, g0:g0 + 2, :].rearrange("p g (e c) -> p (g e) c", e=E),
                        slot[:, half, p * n:p * n + n].unsqueeze(2).broadcast_to([S, n, CAP]),
                        const("iota", S).unsqueeze(1).broadcast_to([S, n, CAP]), ALU.is_equal).then_inc(disp_ready, 1)

            def slots_lo(g):
                dve.wait_ge(ei_hi_ready, g + 1)
                nc.vector.tensor_tensor(slots_of(ei[1], g), dispatched(g), slots_of(ei[0], g).bitcast(F32),
                                        ALU.subtract).then_inc(ei_lo_ready, 1)

            def hidden_lo(e):
                for pair in range(FT // 2):
                    dve.wait_ge(hid_hi, 3 * e + pair + 1)
                    if e >= 2 and pair == 0:
                        dve.wait_ge(y_psum, e - 1)
                    nc.vector.scalar_tensor_tensor(
                        h_lo[e % 2][:, 2 * pair:2 * pair + 2, :].rearrange("p t s -> p (t s)"),
                        ps[:, 3 * (e % 2) + pair, 0:2 * SLOTS], 0.0,
                        h_hi[e % 2][:, 2 * pair:2 * pair + 2, :].rearrange("p t s -> p (t s)").bitcast(F32),
                        ALU.max, ALU.subtract).then_inc(hid_lo, 1)

            def split_in_b(e):
                dve.wait_ge(wi_hi, e + 1)
                nc.vector.tensor_tensor(w_b[e % 2][DB:128, :], raw_b[:, e % 2, :], w_b[e % 2][0:DB, :].bitcast(F32),
                                        ALU.subtract).then_inc(wi_b_lo, 1)

            def hold_y(e):
                dve.wait_ge(y_low_held, e + 1)
                if e >= 2:
                    dve.wait_ge(y_moved[e % 2], 16 * GH * (e // 2))
                nc.vector.tensor_tensor(y[:, e % 2], ps[0:HS, 6:8, 0:D], y_low[:], ALU.add).then_inc(y_held, 1)

            nc.vector.memset(filler[:], 1.0).then_inc(filler_ready, 1)
            dve.wait_ge(small_loaded, 16)
            at = SMALL["wqk"][0]
            for j in range(4):
                nc.vector.tensor_scalar(blk[:, j, :], const("mask"), small[:, at + j:at + j + 1], SCALE, ALU.mult,
                                        ALU.mult).then_inc(blk_ready, 1)
            norm_stats(0)
            norm_apply(0)
            norm_stats(1)
            turned1(0)
            turned1(1)
            norm_apply(1)
            turned1(2)
            turned1(3)
            norm_stats(2)
            norm_apply(2)
            softmax_shift(0, 0)
            softmax_sum(0, 0)
            norm_stats(3)
            softmax_mean(0, 0)
            turned1(4)
            turned1(5)
            norm_apply(3)
            softmax_shift(1, 0)
            turned1(6)
            turned1(7)
            softmax_sum(1, 0)
            softmax_mean(1, 0)
            dve.wait_ge(tables_loaded, 16)
            nc.vector.tensor_copy(tri[:], const("tri", S)).then_inc(cast_ready, 1)
            nc.vector.tensor_copy(ones[:], const("ones", S)).then_inc(cast_ready, 1)
            split_in_b(0)
            softmax_shift(0, 1)
            softmax_sum(0, 1)
            softmax_mean(0, 1)
            norm_stats(4)
            softmax_shift(1, 1)
            norm_stats(5)
            softmax_sum(1, 1)
            norm_apply(4)
            softmax_mean(1, 1)
            norm_apply(5)
            split_in_b(1)
            norm_stats(6)
            norm_stats(7)
            norm_apply(6)
            route_shifts(0)
            norm_apply(7)
            route_first(0)
            route_second(0)
            route_slots(0)
            route_shifts(1)
            route_first(1)
            route_second(1)
            slots_lo(0)
            slots_lo(1)
            route_slots(1)
            slots_lo(2)
            slots_lo(3)
            for g in range(4, 8):
                slots_lo(g)
            hidden_lo(0)
            for e in range(E):
                if e + 2 < E:
                    split_in_b(e + 2)
                if e + 1 < E:
                    hidden_lo(e + 1)
                hold_y(e)
            for p in range(4):
                dve.wait_ge(mix_psum, p + 1)
                for i in range(2):
                    g = 2 * p + i
                    nc.vector.tensor_tensor(res[:, g, :], ps[0:S, p, i * 256:i * 256 + D], h[:, g, :], ALU.add).then_inc(res_ready, 1)

        @block.gpsimd
        def _(pool):
            def inverse_std(p):
                gs = slice(2 * (p % GH), 2 * (p % GH) + 2)
                pool.wait_ge(ln_moments, 2 * p + 2)
                nc.gpsimd.tensor_tensor(var[:, gs], moments[:, gs, 1], const("eps", S), ALU.add).then_inc(ln_var, 1)
                pool.wait_ge(ln_var, p + 1)
                nc.gpsimd.tensor_tensor(rstd[:, gs], var[:, gs], const("power", S), ALU.pow).then_inc(ln_rstd, 1)

            def weigh(stage, half):
                pool.wait_ge(att_exp[stage], half + 1)
                src = "qk"[stage]
                pool.wait_ge(proj_held[src], half + 1)
                if stage == 1:
                    pool.wait_ge(att_logits[1], half + 1)
                nc.gpsimd.tensor_tensor(att[half]["w"][:], att[half]["e"][:], att[half][src][:], ALU.mult)\
                    .then_inc(att_weighted[stage], 1)

            def split_qkv(j):
                cols = slice(QKV_J * j, QKV_J * j + QKV_J)
                pool.wait_ge(qkv_hi, j + 1)
                nc.gpsimd.tensor_tensor(wqkv_lo[:, :, cols], wqkv[:, :, cols], wqkv_hi[:, :, cols].bitcast(F32),
                                        ALU.subtract).then_inc(qkv_lo, 1)

            def bias(p):
                pool.wait_ge(xn_ready, 2 * p + 2)
                gs = slice(2 * p, 2 * p + 2)
                nc.gpsimd.tensor_tensor(h[:, gs, :], h[:, gs, :], const("bp", S).unsqueeze(1).broadcast_to([S, 2, D]),
                                        ALU.add).then_inc(biased, 1)

            def split(e, hi, done, a, b):
                pool.wait_ge(hi, e + 1)
                nc.gpsimd.tensor_tensor(w[e % 2][:, 1, a:b], raw[:, e % 2, a:b], w[e % 2][:, 0, a:b].bitcast(F32),
                                        ALU.subtract).then_inc(done, 1)

            def split_in(e):
                split(e, wi_hi, wi_lo, 0, WO)

            def split_out(e):
                split(e, wo_hi, wo_lo, WO, WEXP)

            def split_x(p):
                pool.wait_ge(x_hi_ready, p + 1)
                gs = slice(2 * p, 2 * p + 2)
                nc.gpsimd.tensor_tensor(x_lo[:, gs, 0:D], xn[:, gs, :], x_hi[:, gs, 0:D].bitcast(F32), ALU.subtract)
                nc.gpsimd.tensor_tensor(x_lo[:, gs, D:], xn[:, gs, DA:], x_hi[:, gs, D:].bitcast(F32), ALU.subtract)\
                    .then_inc(x_lo_ready, 1)

            def gates(half):
                gs = slice(GH * half, GH * half + GH)
                n = GH * E
                pool.wait_ge(rsum_ready, half + 1)
                pool.wait_ge(choice_ready, half + 1)
                nc.gpsimd.tensor_tensor(gate[:, half, 0, :], chosen[:, half, 0, :], chosen[:, half, 1, :], ALU.add)\
                    .then_inc(gate_step, 1)
                nc.gpsimd.tensor_tensor(gate[:, half, 1, :].rearrange("p (g e) -> p g e", g=GH), ex[:, gs, :],
                                        cols[:, half, 2, :].unsqueeze(2).broadcast_to([S, GH, E]), ALU.mult)\
                    .then_inc(gate_step, 1)
                pool.wait_ge(gate_step, 3 * half + 2)
                nc.gpsimd.tensor_tensor(gate[:, half, 2, :], gate[:, half, 0, :], gate[:, half, 1, :], ALU.mult)\
                    .then_inc(gate_step, 1)
                pool.wait_ge(gate_step, 3 * half + 3)
                pool.wait_ge(disp_ready, 2 * half + 2)
                nc.gpsimd.tensor_tensor(comb[:, gs, :].rearrange("p g (e c) -> p (g e) c", e=E),
                                        disp[:, gs, :].rearrange("p g (e c) -> p (g e) c", e=E).bitcast(F32),
                                        gate[:, half, 2, :].unsqueeze(2).broadcast_to([S, n, CAP]), ALU.mult)\
                    .then_inc(comb_ready, 1)
                pool.wait_ge(comb_ready, half + 1)
                own = comb7[:, gs, :].rearrange("p g n -> p (g n)")
                for g in range(GH):
                    at = g * (HS + CAP)
                    last = nc.gpsimd.tensor_copy(own[:, at:at + CAP], comb[:, GH * half + g, EC - CAP:EC])
                last.then_inc(comb7_ready, 1)

            nc.gpsimd.memset(comb7[:], 0.0).then_inc(comb7_zero, 1)
            pool.wait_ge(comb7_zero, 1)
            pool.wait_ge(small_loaded, 16)
            inverse_std(0)
            split_qkv(0)
            inverse_std(1)
            split_qkv(1)
            split_qkv(2)
            inverse_std(2)
            pool.wait_ge(tables_loaded, 16)
            bias(0)
            bias(1)
            weigh(0, 0)
            inverse_std(3)
            bias(2)
            weigh(1, 0)
            bias(3)
            split_in(0)
            weigh(0, 1)
            split_out(0)
            inverse_std(4)
            weigh(1, 1)
            inverse_std(5)
            split_x(0)
            split_x(1)
            inverse_std(6)
            inverse_std(7)
            split_in(1)
            split_x(2)
            split_x(3)
            gates(0)
            gates(1)
            for e in range(E - 1):
                if e + 2 < E:
                    split_in(e + 2)
                split_out(e + 1)


def kernel(**inputs):
    import concourse.bacc as _bacc
    from concourse.bass_utils import run_bass_kernel_spmd as _run

    a = {k: np.asarray(v) for k, v in inputs.items()}
    f32 = np.float32

    xi = a["x"].reshape(IMAGES, 3, 7, 16, 7, 16).transpose(3, 5, 1, 0, 2, 4).reshape(KT, 128, 4, 2 * S)
    xi = np.ascontiguousarray(xi.transpose(2, 1, 0, 3)).reshape(4, 128, KT * 2 * S)
    wt = np.ascontiguousarray(a["L0_tok_W_lin"].T.reshape(KT, 128, D).transpose(1, 0, 2)).reshape(128, KT * D)

    wq = a["L0_attn_Wqkv"].T
    wqkv = np.zeros((128, 2, QKV_W), f32)
    for k, rows in enumerate((slice(0, DA), slice(DA, D))):
        n = rows.stop - rows.start
        for j in range(3):
            at = QKV_J * j
            wqkv[:n, k, at:at + DA] = wq[rows, D * j:D * j + DA]
            wqkv[:n, k, at + DA + DB:at + DA + 2 * DB] = wq[rows, D * j + DA:D * j + D]
    wqkv[DB:, 1] = wqkv[:DB, 1]

    small = np.zeros((128, SMALL_W), f32)

    def put(name, value):
        at, w = SMALL[name]
        value = np.asarray(value)
        small[:value.shape[0], at:at + w] = value

    put("bias", np.broadcast_to(a["L0_tok_b_lin"], (128, D)))
    head = np.arange(128) // HD
    put("bp", np.broadcast_to(a["L0_attn_bp"], (128, D)))
    put("mask", (head[:, None] == head[None, :]).astype(f32))
    wqv, wkv = a["L0_attn_w_q"].reshape(D), a["L0_attn_w_k"].reshape(D)
    put("wqk", np.stack([wqv[:DA], np.tile(wqv[DA:], 2), wkv[:DA], np.tile(wkv[DA:], 2)], axis=1))
    put("ident", np.eye(128, dtype=f32))
    wp = a["L0_attn_Wp"].T
    put("wp_a", wp[:DA])
    put("wp_b", np.concatenate([wp[DA:], wp[DA:]]))
    put("router_a", a["L0_ffn_w_router"][:DA])
    put("router_b", a["L0_ffn_w_router"][DA:])
    put("tri", np.triu(np.ones((S, S), f32)))
    put("ones", np.ones((S, S), f32))
    put("rank", np.broadcast_to(np.tile(E - np.arange(E, dtype=f32), GH), (S, GH * E)))
    put("iota", np.broadcast_to(np.arange(1, CAP + 1, dtype=f32), (S, CAP)))

    put("eps", np.full((S, 2), EPS, f32))
    put("power", np.full((S, 2), -0.5, f32))

    wi, wo = a["L0_ffn_wi"], a["L0_ffn_wo"]
    wexp = np.empty((E, 128, WEXP), f32)
    wexp[:, :, 0:F] = wi[:, :DA]
    wexp[:, :, WO:] = wo.reshape(E, FT, 128, D).transpose(0, 2, 1, 3).reshape(E, 128, FT * D)
    wexp_b = np.ascontiguousarray(wi[:, DA:])

    arrays = {"x_dram": xi, "wtok_dram": wt, "wqkv_dram": wqkv.reshape(128, 2 * QKV_W), "small_dram": small,
              "wexp_dram": wexp, "wexp_b_dram": wexp_b}
    nc = _bacc.Bacc("TRN2", target_bir_lowering=False, num_devices=1)
    args = [nc.dram_tensor(k, v.shape, F32, kind="ExternalInput").ap() for k, v in arrays.items()]
    out = nc.dram_tensor("out_0_dram", (IMAGES * N_TOK, D), F32, kind="ExternalOutput").ap()
    build(nc, *args, out)
    r = _run(nc, [arrays], core_ids=[0])
    return r.results[0]["out_0_dram"].reshape(IMAGES, N_TOK, D)
```

```python
from contextlib import ExitStack

import numpy as np

import concourse.bass as bass
from concourse import mybir

F32 = mybir.dt.float32
F32R = mybir.dt.float32r
BF16 = mybir.dt.bfloat16
ALU = mybir.AluOpType
ACT = mybir.ActivationFunctionType
AX = mybir.AxisListType

IMAGES, N_TOK, D = 16, 49, 192
PATCH = 768
KT = PATCH // 128
HEADS, HD = 12, 16
SCALE = float(HD) ** -0.5
EPS = 1e-5
E, F, CAP = 8, 768, 30
G, S = 8, 98
GH = G // 2
TH = GH * S
DA, DB = 128, 64
FT = F // 128
HS = GH * CAP
SLOTS = G * CAP
EC = E * CAP

NB = 12
B_COLS = 4 * N_TOK
A_COLS = 2 * B_COLS

QKV_J = DA + DB + DB + DB
QKV_W = 3 * QKV_J
SMALL = {}


def _place(name, width, at=[0]):
    SMALL[name] = (at[0], width)
    at[0] += width


_place("bias", D)
_place("ident", 128)
_place("eps", 2)
_place("power", 2)
_place("minus", 2)
_place("mask", 128)
_place("wqk", 4)
SMALL_FIRST = SMALL["wqk"][0] + SMALL["wqk"][1]
_place("bp", D)
_place("wp_a", D)
_place("wp_b", D)
_place("router_a", E)
_place("router_b", E)
_place("tri", S)
_place("ones", S)
_place("rank", GH * E)
_place("iota", CAP)
SMALL_W = sum(w for _, w in SMALL.values())

WO = F
WEXP = WO + FT * D


def build(nc, x_in, wtok_in, wqkv_in, small_in, wexp_in, wexp_b_in, out):
    ctx = ExitStack()
    with ctx:
        def sb(name, shape, dt=F32, scope=ctx):
            return scope.enter_context(nc.sbuf_tensor(name, shape, dt))

        def sem(name):
            return ctx.enter_context(nc.semaphore(name))

        ps = ctx.enter_context(nc.psum_tensor("ps", [128, 8, 512], F32))

        small = sb("small", [128, SMALL_W])

        def const(name, rows=128):
            at, w = SMALL[name]
            return small[0:rows, at:at + w]

        filler = sb("filler", [128, 512], BF16)
        tri = sb("tri", [S, S], BF16)
        ones = sb("ones", [S, S], BF16)
        blk = sb("blk", [128, 4, 128])
        h = sb("h", [S, G, D])
        xn = sb("xn", [S, G, D])
        stats = sb("stats", [S, G, 6])
        moments = sb("moments", [S, G, 2])
        var = sb("var", [S, G])
        rstd = sb("rstd", [S, G])
        minus_mean = sb("minus_mean", [S, G])
        ln_bias = sb("ln_bias", [S, G])
        ACT_NORMS = (3, 4, 5)
        xn2t_a = sb("xn2t_a", [128, G, S])
        xn2t_b = sb("xn2t_b", [DB, G, S])
        x_lo = sb("x_lo", [S, G, D + DB], F32R)
        shifted = sb("shifted", [S, G, E])
        ex = sb("ex", [S, G, E])
        ex2 = sb("ex2", [S, G, E])
        ranked = sb("ranked", [S, G, E])
        ranked2 = sb("ranked2", [S, G, E])
        chosen = sb("chosen", [S, 2, 2, GH * E], BF16)
        slot2 = sb("slot2", [S, 2, 2, GH * E])
        slot = sb("slot", [S, 2, GH * E])
        gate = sb("gate", [S, 2, 3, GH * E])
        cols = sb("cols", [S, 2, 6, GH])
        disp = sb("disp", [S, G, EC], F32R)
        comb = sb("comb", [S, G, EC])
        comb7 = sb("comb7", [S, 2, GH * (HS + CAP)])
        embedding_parts = ExitStack()
        x_part = [sb(f"x_part_{p}", [128, 2, KT, 2 * S], F32R, embedding_parts) for p in ("hi", "lo")]
        wtok_part = [sb(f"wtok_part_{p}", [128, KT, D], F32R, embedding_parts) for p in ("hi", "lo")]
        embedding_parts.close()
        ei = [sb(f"ei_{p}", [128, 2, E, SLOTS], F32R) for p in ("hi", "lo")]
        raw = sb("raw", [128, 2, WEXP])
        raw_b = sb("raw_b", [DB, 2, F])
        w = [sb(f"wexp{i}", [128, 2, WEXP], F32R) for i in range(2)]
        w_b = [sb(f"wexp_b{i}", [128, F], F32R) for i in range(2)]

        early = ExitStack()
        wqkv_hi = sb("wqkv_hi", [128, 2, QKV_W], F32R, early)
        wqkv_lo = sb("wqkv_lo", [128, 2, QKV_W], F32R, early)
        xnt_a = [sb(f"xnt_a_{p}", [128, G * S], F32R, early) for p in ("hi", "lo")]
        xnt_b = sb("xnt_b", [128, G * S], F32R, early)
        acol = sb("acol", [128, 2, 2, 5, NB], F32, early)

        def attention_tensors(half, names):
            return {n: sb(f"{n}{half}", [128, NB, N_TOK], F32, early) for n in names}

        att = [attention_tensors(0, "q"), attention_tensors(1, "")]
        unsplit = ExitStack()
        wqkv = sb("wqkv", [128, 2, QKV_W], F32, unsplit)
        unsplit.close()
        att[0].update(attention_tensors(0, "kvew"))
        embedding = ExitStack()
        x = sb("x", [128, 4, KT, 2 * S], F32, embedding)
        wtok = sb("wtok", [128, KT, D], F32, embedding)
        embedding.close()
        att[1].update(attention_tensors(1, "qkvew"))
        x_hi = sb("x_hi", [S, G, D + DB], F32R, early)
        early.close()
        h_hi = [sb(f"h_hi{i}", [128, FT, SLOTS], F32R) for i in range(2)]
        h_lo = [sb(f"h_lo{i}", [128, FT, SLOTS], F32R) for i in range(2)]
        y = sb("y", [HS, 2, 2, D])
        y_all = sb("y_all", [HS, 2, G, D])
        res = sb("res", [S, G, D])
        combT = sb("combT", [HS, G, 2, S])
        comb7T = sb("comb7T", [HS, G, S])
        y_low = sb("y_low", [HS, 2, D])

        x_loaded = [sem(f"x_loaded{c}") for c in range(5)]
        wtok_loaded = [sem(f"wtok_loaded{c}") for c in range(2)]
        x_part_hi = sem("x_part_hi")
        x_part_lo = sem("x_part_lo")
        wtok_hi = sem("wtok_hi")
        wtok_lo = sem("wtok_lo")
        filler_ready = sem("filler_ready")
        small_loaded = sem("small_loaded")
        wqkv_loaded = sem("wqkv_loaded")
        tables_loaded = sem("tables_loaded")
        qkv_hi = sem("qkv_hi")
        qkv_lo = sem("qkv_lo")
        biased = sem("biased")
        cast_ready = sem("cast_ready")
        blk_ready = sem("blk_ready")
        tok_ready = sem("tok_ready")
        added = sem("added")
        ln_stats = sem("ln_stats")
        ln_moments = sem("ln_moments")
        ln_var = sem("ln_var")
        ln_rstd = sem("ln_rstd")
        ln_minus = sem("ln_minus")
        ln_bias_ready = sem("ln_bias_ready")
        xn_by_dve = sem("xn_by_dve")
        xn_by_act = sem("xn_by_act")
        tr_ready = sem("tr_ready")
        xnt_hi_ready = sem("xnt_hi_ready")
        xnt_lo_ready = sem("xnt_lo_ready")
        proj_ready = {j: sem(f"{j}_ready") for j in "qkv"}
        proj_held = {j: sem(f"{j}_held") for j in "qkv"}
        att_logits = [sem(f"att_logits{a}") for a in (1, 2)]
        att_max = [sem(f"att_max{a}") for a in (1, 2)]
        att_shift = [sem(f"att_shift{a}") for a in (1, 2)]
        att_exp = [sem(f"att_exp{a}") for a in (1, 2)]
        att_sum = [sem(f"att_sum{a}") for a in (1, 2)]
        att_weighted = [sem(f"att_weighted{a}") for a in (1, 2)]
        att_wsum = [sem(f"att_wsum{a}") for a in (1, 2)]
        att_rsum = [sem(f"att_rsum{a}") for a in (1, 2)]
        att_glob = [sem(f"att_glob{a}") for a in (1, 2)]
        kq_ready = sem("kq_ready")
        u_ready = sem("u_ready")
        attn_out = sem("attn_out")
        tr2_ready = sem("tr2_ready")
        xn2t_ready = sem("xn2t_ready")
        router_ready = sem("router_ready")
        x_hi_ready = sem("x_hi_ready")
        x_lo_ready = sem("x_lo_ready")
        route_step = sem("route_step")
        route_exp = sem("route_exp")
        route_shift = sem("route_shift")
        first_ready = sem("first_ready")
        choice_ready = sem("choice_ready")
        cum_ready = sem("cum_ready")
        cum_used = sem("cum_used")
        slot_ready = sem("slot_ready")
        disp_ready = sem("disp_ready")
        rsum_ready = sem("rsum_ready")
        gate_step = sem("gate_step")
        comb_ready = sem("comb_ready")
        ei_hi_psum = sem("ei_hi_psum")
        ei_lo_psum = sem("ei_lo_psum")
        ei_hi_ready = sem("ei_hi_ready")
        ei_lo_ready = [sem(f"ei_lo_ready{i}") for i in range(2)]
        combT_psum = sem("combT_psum")
        combT_ready = sem("combT_ready")
        comb7_zero = sem("comb7_zero")
        comb7_ready = sem("comb7_ready")
        comb7T_psum = sem("comb7T_psum")
        comb7T_ready = sem("comb7T_ready")
        y_low_held = sem("y_low_held")
        wi_loaded = [sem(f"wi_loaded{i}") for i in range(2)]
        wo_loaded = [sem(f"wo_loaded{i}") for i in range(2)]
        wi_hi = sem("wi_hi")
        wi_lo = sem("wi_lo")
        wi_b_lo = sem("wi_b_lo")
        wo_hi = sem("wo_hi")
        wo_lo = sem("wo_lo")
        hid_psum = sem("hid_psum")
        hid_hi = sem("hid_hi")
        hid_lo = sem("hid_lo")
        y_psum = sem("y_psum")
        y_held = sem("y_held")
        y_moved = [sem(f"y_moved{i}") for i in range(2)]
        mix_psum = sem("mix_psum")
        res_ready = sem("res_ready")
        stored = sem("stored")

        block = ctx.enter_context(nc.Block())

        def blocks(bank):
            quads = ps[:, bank:bank + 2, :].rearrange("p b (h c) -> p (b h) c", h=2)[:, 0:NB // 4, 0:B_COLS]
            return quads.rearrange("p b (s n) -> p b s n", n=N_TOK)

        def a_blocks(bank):
            return ps[:, bank, :].rearrange("p (h c) -> p h c", h=2)[:, :, 0:B_COLS]

        def quads(t):
            return t.rearrange("p (b s) n -> p b s n", b=NB // 4)

        def spread(col):
            return col.rearrange("p (b s) -> p b s", b=NB // 4).unsqueeze(3).broadcast_to([128, NB // 4, 4, N_TOK])

        def normed(g, norm):
            p = norm * GH + g // 2
            by_act = [n in ACT_NORMS for n in range(p + 1)]
            return (xn_by_act, xn_by_dve)[not by_act[p]], 2 * (by_act.count(by_act[p]) - 1) + g % 2 + 1

        EMBED_BANK = 0
        TURN_BANK = 2
        PROJ_BANK = {"q": (4, 0), "k": (6, 6), "v": (4, 0)}
        LOGIT_BANK = ((2, 2), (6, 6))
        OUT_BANK = (4, 0)
        DISP_BANK = (4, 6, 2)
        Y_BANK = (6, 0)
        MIX_BANK = 2
        COMBT_BANK = (2, 6)
        COMB7T_BANK = 4

        def y_banks(e):
            bank = Y_BANK[e == E - 1]
            return ps[0:HS, bank:bank + 2, :]

        def dispatched(g, part):
            return ps[:, DISP_BANK[g % 3] + part, 0:2 * EC].rearrange("p (k e c) -> p k e c", k=2, e=E)

        def slots_of(t, g):
            return t[:, :, :, g * CAP:g * CAP + CAP]

        @block.sync
        def _(sp):
            half_k = KT // 2
            wtok_v = wtok_in.rearrange("p (k d) -> p k d", k=KT)
            x_v = x_in.rearrange("c p (k t) -> c p k t", k=KT)
            for k in (0, half_k):
                sp.dma_start(wtok[:, k:k + half_k, :], wtok_v[:, k:k + half_k, :]).then_inc(wtok_loaded[k // half_k], 16)
                sp.dma_start(x[:, 0, k:k + half_k], x_v[0, :, k:k + half_k]).then_inc(x_loaded[k // half_k], 16)
            sp.dma_start(small[:, 0:SMALL_FIRST], small_in[:, 0:SMALL_FIRST]).then_inc(small_loaded, 16)
            sp.dma_start(x[:, 1], x_v[1]).then_inc(x_loaded[2], 16)
            sp.dma_start(x[:, 2], x_v[2]).then_inc(x_loaded[3], 16)
            sp.dma_start(wqkv[:].rearrange("p k d -> p (k d)"), wqkv_in).then_inc(wqkv_loaded, 16)
            sp.dma_start(x[:, 3], x_v[3]).then_inc(x_loaded[4], 16)
            sp.dma_start(small[:, SMALL_FIRST:], small_in[:, SMALL_FIRST:]).then_inc(tables_loaded, 16)

            def load_in(e):
                if e >= 2:
                    sp.wait_ge(wi_hi, e - 1)
                    sp.wait_ge(wi_lo, e - 1)
                    sp.wait_ge(wi_b_lo, e - 1)
                sp.dma_start(raw[:, e % 2, 0:WO], wexp_in[e, :, 0:WO]).then_inc(wi_loaded[e % 2], 16)
                sp.dma_start(raw_b[:, e % 2, :], wexp_b_in[e]).then_inc(wi_loaded[e % 2], 16)

            def load_out(e):
                if e >= 2:
                    sp.wait_ge(wo_hi, e - 1)
                    sp.wait_ge(wo_lo, e - 1)
                sp.dma_start(raw[:, e % 2, WO:WEXP], wexp_in[e, :, WO:WEXP]).then_inc(wo_loaded[e % 2], 16)

            def move_y(e):
                sp.wait_ge(y_held, e + 1)
                dst = y_all[CAP * (e % 4):CAP * (e % 4) + CAP, e // 4].rearrange("c (h g) d -> c h g d", h=2)
                for g in range(GH):
                    sp.dma_start(dst[:, :, g, :], y[g * CAP:g * CAP + CAP, e % 2]).then_inc(y_moved[e % 2], 16)

            for e in range(3):
                load_in(e)
                load_out(e)
            load_in(3)
            for e in range(E - 1):
                if e + 4 < E:
                    load_in(e + 4)
                if e + 3 < E:
                    load_out(e + 3)
                move_y(e)
            for p in range(G // 2):
                sp.wait_ge(res_ready, p + 1)
                rows = out[2 * p * S:2 * (p + 1) * S, :].rearrange("(g s) d -> s g d", g=2)
                sp.dma_start(rows, res[:, 2 * p:2 * p + 2, :]).then_inc(stored, 16)
            sp.wait_ge(stored, 16 * (G // 2))

        @block.tensor
        def _(pe):
            def mm(o, a, b, first, last):
                return nc.tensor.matmul(o, a, b, start=first, stop=last)

            def mm3(o, a, b, first, last):
                mm(o, a[0], b[0], first, False)
                mm(o, a[0], b[1], False, False)
                return mm(o, a[1], b[0], False, last)

            def embed(g):
                if g > 0 and g % 2 == 0:
                    pe.wait_ge(x_loaded[g // 2 + 1], 16)
                if g >= 2:
                    pe.wait_ge(added, g - 1)
                for k in range(KT):
                    if g == 0 and k % (KT // 2) == 0:
                        pe.wait_ge(wtok_loaded[k // (KT // 2)], 16)
                        pe.wait_ge(x_loaded[k // (KT // 2)], 16)
                    last = mm(ps[0:S, EMBED_BANK + g % 2, 0:D], x[:, g // 2, k, (g % 2) * S:(g % 2) * S + S],
                              wtok[:, k, :], k == 0, k == KT - 1)
                last.then_inc(tok_ready, 1)

            def embed_parts(g):
                pe.wait_ge(x_part_lo, g // 2 - 1)
                pe.wait_ge(wtok_lo, 1)
                pe.wait_ge(added, g - 1)
                for k in range(KT):
                    last = mm3(ps[0:S, EMBED_BANK + g % 2, 0:D],
                               [p[:, g // 2 - 2, k, (g % 2) * S:(g % 2) * S + S] for p in x_part],
                               [p[:, k, :] for p in wtok_part], k == 0, k == KT - 1)
                last.then_inc(tok_ready, 1)

            def transposed(g, done):
                b = TURN_BANK + g % 2
                nc.tensor.transpose(ps[0:DA, b, 0:S], xn[:, g, 0:DA], const("ident", S)[:, 0:S])
                nc.tensor.transpose(ps[0:DB, b, 128:128 + S], xn[:, g, DA:D], const("ident", S)[:, 0:S]).then_inc(done, 1)

            def turn(g):
                pe.wait_ge(*normed(g, 0))
                if g in (4, 5):
                    pe.wait_ge(att_shift[0], 1)
                elif g >= 2:
                    pe.wait_ge(xnt_lo_ready, g - 1)
                transposed(g, tr_ready)

            def project(j, half):
                bank = PROJ_BANK[j][half]
                pe.wait_ge(xnt_lo_ready, GH * (half + 1))
                if (j, half) == ("q", 1):
                    pe.wait_ge(added, G)
                elif (j, half) == ("k", 1):
                    pe.wait_ge(att_shift[1], 1)
                elif j == "v":
                    pe.wait_ge(proj_held["q"], half + 1)
                n = "qkv".index(j)
                if half == 0:
                    pe.wait_ge(qkv_lo, 1 if j == "q" else 3)
                w0 = QKV_J * n
                t0 = TH * half

                def product(o, at, tokens, first, last):
                    hi, lo = (t[:, :, w0 + at:w0 + at + 128] for t in (wqkv_hi, wqkv_lo))
                    x_a, x_b = [t[:, tokens] for t in xnt_a], xnt_b[:, tokens]
                    mm3(o, (hi[:, 0, :], lo[:, 0, :]), x_a, first, False)
                    mm(o, hi[:, 1, :], x_b, False, False)
                    return mm(o, lo[:, 1, :], x_b, False, last)

                product(a_blocks(bank), 0, slice(t0, t0 + A_COLS), True, True)
                o = ps[:, bank + 1, 0:B_COLS]
                product(o, DA + DB, slice(t0, t0 + B_COLS), True, False)
                product(o, DA, slice(t0 + B_COLS, t0 + A_COLS), False, True).then_inc(proj_ready[j], 1)

            def logits(stage, half):
                bank = LOGIT_BANK[stage][half]
                if stage == 0:
                    pe.wait_ge(blk_ready, 4)
                    pe.wait_ge(xnt_lo_ready, GH * (half + 1))
                    pe.wait_ge(proj_held["q"], half + 1)
                    src = att[half]["q"]
                else:
                    pe.wait_ge(proj_held["k"], half + 1)
                    pe.wait_ge(kq_ready, half + 1)
                    src = att[half]["w"]
                src = src[:].rearrange("p s n -> p (s n)")
                mm(a_blocks(bank), blk[:, 2 * stage, :], src[:, 0:A_COLS], True, True)
                mm(ps[:, bank + 1, 0:B_COLS], blk[:, 2 * stage + 1, :], src[:, A_COLS:], True,
                   True).then_inc(att_logits[stage], 1)

            def fill(n, bank=7):
                for _ in range(n):
                    mm(ps[:, bank, :], filler[:, 0:128], filler[:], True, True)

            def acc(o, a, b, first, last):
                return nc.tensor.matmul(o, a, b, start=first, stop=last, skip_group_check=True)

            def out_operands(t, g):
                t = t[:].rearrange("p s n -> p (s n)")
                r, c = DB * (g // 2), A_COLS + g % 2 * S
                return t[:, g * S:g * S + S], t[r:r + DB, c:c + S], r

            def residual_q(half):
                bank = OUT_BANK[half]
                pe.wait_ge(proj_held["v"], half + 1)
                for g in range(GH):
                    q_a, q_b, r = out_operands(att[half]["q"], g)
                    o = ps[0:S, bank + g // 2, g % 2 * D:g % 2 * D + D]
                    acc(o[:, 0:DA], q_a, const("ident"), g % 2 == 0, False)
                    acc(o[:, DA:D], q_b, const("ident")[r:r + DB, r:r + DB], False, False)

            def attention_out(half):
                bank = OUT_BANK[half]
                pe.wait_ge(u_ready, half + 1)
                for g in range(GH):
                    o = ps[0:S, bank + g // 2, g % 2 * D:g % 2 * D + D]
                    u_a, u_b, r = out_operands(att[half]["w"], g)
                    acc(o, u_a, const("wp_a"), False, False)
                    last = acc(o, u_b, const("wp_b")[r:r + DB, :], False, g % 2 == 1)
                    if g % 2 == 1:
                        last.then_inc(attn_out, 1)

            def turn2(g):
                pe.wait_ge(*normed(g, 1))
                if g < 2:
                    pe.wait_ge(att_shift[0], 2)
                else:
                    pe.wait_ge(xn2t_ready, g - 1)
                transposed(g, tr2_ready)

            def router(p):
                for gg in (2 * p, 2 * p + 1):
                    pe.wait_ge(xn2t_ready, gg + 1)
                    at = gg % GH * E
                    o = ps[0:S, OUT_BANK[p // 2], at:at + E]
                    mm(o, xn2t_a[:, gg, :], const("router_a"), True, False)
                    last = mm(o, xn2t_b[:, gg, :], const("router_b", DB), False, True)
                last.then_inc(router_ready, 1)

            def cumulate(half):
                bank = OUT_BANK[half] + 1
                pe.wait_ge(first_ready, half + 1)
                mm(ps[0:S, bank, 0:GH * E], tri[:], chosen[:, half, 0, :], True, True)
                mm(ps[0:S, bank, GH * E:2 * GH * E], ones[:], chosen[:, half, 0, :], True, False)
                pe.wait_ge(choice_ready, half + 1)
                mm(ps[0:S, bank, GH * E:2 * GH * E], tri[:], chosen[:, half, 1, :], False, True).then_inc(cum_ready, 1)

            def dispatch(g):
                pe.wait_ge(x_lo_ready, g // 2 + 1)
                pe.wait_ge(disp_ready, g // 2 + 1)
                if g == 0:
                    pe.wait_ge(cum_used, 1)
                elif g == 2:
                    pe.wait_ge(xn2t_ready, G)
                elif g >= 3:
                    pe.wait_ge(ei_hi_ready, g - 2)
                    pe.wait_ge(ei_lo_ready[(g - 3) // GH], (g - 3) % GH + 1)
                for i, (part, done) in enumerate(((x_hi, ei_hi_psum), (x_lo, ei_lo_psum))):
                    for c in range(2):
                        last = mm(ps[:, DISP_BANK[g % 3] + i, c * EC:c * EC + EC], part[:, g, c * 128:c * 128 + 128],
                                  disp[:, g, :], True, True)
                    last.then_inc(done, 1)

            def turn_comb(half):
                pe.wait_ge(comb_ready, half + 1)
                if half == 0:
                    pe.wait_ge(ei_hi_ready, GH + 2)
                    pe.wait_ge(ei_lo_ready[1], 2)
                for q in range(4):
                    g = GH * half + q
                    b = COMBT_BANK[half] + q // 2
                    for s in range(2):
                        c = (q % 2 * 2 + s) * 128
                        rows = (HS, HS - CAP)[s]
                        last = nc.tensor.transpose(ps[0:rows, b, c:c + S], comb[:, g, s * HS:s * HS + rows],
                                                   const("ident", S)[:, 0:S])
                last.then_inc(combT_psum, 1)

            def turn_comb7():
                pe.wait_ge(comb7_ready, 2)
                for g in range(G):
                    last = nc.tensor.transpose(ps[0:HS, COMB7T_BANK + g // GH, g % GH * 128:g % GH * 128 + S],
                                               comb7[:, g // GH, g % GH * HS:g % GH * HS + HS], const("ident", S)[:, 0:S])
                last.then_inc(comb7T_psum, 1)

            def expert_in(e, pairs=range(FT // 2)):
                pe.wait_ge(wi_hi, e + 1)
                pe.wait_ge(wi_lo, e + 1)
                pe.wait_ge(wi_b_lo, e + 1)
                buf = e % 2
                for pair in pairs:
                    for t in range(2):
                        f = 2 * pair + t
                        o = ps[:, 3 * buf + pair, t * SLOTS:t * SLOTS + SLOTS]
                        mm3(o, [w[buf][:, p, f * 128:f * 128 + 128] for p in range(2)], [p[:, 0, e, :] for p in ei], True, False)
                        mm(o, w_b[buf][:, f * 128:f * 128 + 128], ei[0][:, 1, e, :], False, False)
                        last = mm(o, w_b[buf][:, f * 128:f * 128 + 128], ei[1][:, 1, e, :], False, True)
                    last.then_inc(hid_psum, 1)

            def expert_out(e, buf):
                pe.wait_ge(wo_hi, e + 1)
                pe.wait_ge(wo_lo, e + 1)
                pe.wait_ge(hid_hi, 3 * (e + 1))
                pe.wait_ge(hid_lo, 3 * (e + 1))
                for half in range(2):
                    bank = ps[0:HS, Y_BANK[e == E - 1] + half, 0:2 * D]
                    for f in range(FT):
                        cols = slice(half * HS, half * HS + HS)
                        wo = w[buf][:, :, WO + f * D:WO + f * D + D]
                        acc(bank.rearrange("p (h d) -> p h d", h=2), h_hi[buf][:, f, cols], wo, f == 0, False)
                        last = acc(bank[:, 0:D], h_lo[buf][:, f, cols], wo[:, 0, :], False, f == FT - 1)
                last.then_inc(y_psum, 1)

            def mixed(g):
                return ps[0:S, MIX_BANK + g // 2, g % 2 * 256:g % 2 * 256 + D]

            pe.wait_ge(filler_ready, 1)
            fill(8)
            embed(0)
            embed(1)
            embed(2)
            embed(3)
            pe.wait_ge(small_loaded, 16)
            turn(0)
            turn(1)
            embed_parts(4)
            turn(2)
            turn(3)
            embed_parts(5)
            project("q", 0)
            project("k", 0)
            logits(0, 0)
            embed_parts(6)
            embed_parts(7)
            turn(4)
            turn(5)
            project("v", 0)
            pe.wait_ge(proj_held["k"], 1)
            fill(5)
            turn(6)
            turn(7)
            fill(2)
            logits(1, 0)
            project("q", 1)
            project("k", 1)
            logits(0, 1)
            project("v", 1)
            residual_q(0)
            pe.wait_ge(tables_loaded, 16)
            attention_out(0)
            logits(1, 1)
            residual_q(1)
            pe.wait_ge(att_shift[1], 2)
            fill(3)
            pe.wait_ge(att_exp[1], 2)
            fill(5)
            turn2(0)
            turn2(1)
            fill(2)
            attention_out(1)
            turn2(2)
            turn2(3)
            router(0)
            router(1)
            fill(4)
            turn2(4)
            turn2(5)
            turn2(6)
            turn2(7)
            router(2)
            router(3)
            fill(3)
            pe.wait_ge(cast_ready, 2)
            cumulate(0)
            fill(6, 7)
            dispatch(0)
            pe.wait_ge(route_shift, 2)
            fill(1, 0)
            dispatch(1)
            fill(3, 0)
            cumulate(1)
            fill(2, 0)
            dispatch(2)
            fill(1, 0)
            dispatch(3)
            dispatch(4)
            dispatch(5)
            dispatch(6)
            dispatch(7)
            turn_comb(0)
            pe.wait_ge(ei_hi_ready, G)
            pe.wait_ge(ei_lo_ready[0], GH)
            pe.wait_ge(ei_lo_ready[1], GH)
            expert_in(0, (0,))
            turn_comb7()
            expert_in(0, (1,))
            turn_comb(1)
            pe.wait_ge(combT_ready, 1)
            expert_in(0, (2,))
            for e in range(E - 1):
                if e == 0:
                    pe.wait_ge(comb7T_ready, 1)
                else:
                    pe.wait_ge(hid_lo, 3 * e)
                expert_in(e + 1)
                if e == 0:
                    pe.wait_ge(combT_ready, 2)
                else:
                    pe.wait_ge(y_held, e)
                expert_out(e, e % 2)
            pe.wait_ge(hid_lo, 3 * E)
            pe.wait_ge(y_moved[0], 16 * GH * 2)
            pe.wait_ge(y_moved[1], 16 * GH * 2)
            for g in range(G):
                acc(mixed(g), combT[:, g, 0, :], y_all[:, 0, g, :], g % 2 == 0, False)
            expert_out(E - 1, (E - 1) % 2)
            pe.wait_ge(y_moved[0], 16 * GH * 4)
            pe.wait_ge(y_moved[1], 16 * GH * 3)
            n = HS - CAP
            for g in range(G):
                acc(mixed(g), combT[0:n, g, 1, :], y_all[0:n, 1, g, :], False, False)
            pe.wait_ge(y_held, E)
            for g in range(G):
                last = acc(mixed(g), comb7T[:, g, :], y[:, (E - 1) % 2, g // GH, :], False, g % 2 == 1)
                if g % 2 == 1:
                    last.then_inc(mix_psum, 1)

        @block.scalar
        def _(act):
            def copy_turned(g, ready, to_a, to_b, bank, done, count):
                act.wait_ge(ready, count)
                nc.scalar.activation(to_a, ps[0:DA, bank, 0:S], ACT.Copy)
                nc.scalar.activation(to_b, ps[0:DB, bank, 128:128 + S], ACT.Copy).then_inc(done, 1)

            def hold(j, half):
                bank = PROJ_BANK[j][half]
                act.wait_ge(proj_ready[j], half + 1)
                nc.scalar.activation(quads(att[half][j][:]), blocks(bank), ACT.Copy).then_inc(proj_held[j], 1)

            def att_exps(stage, half):
                act.wait_ge(att_shift[stage], half + 1)
                e = att[half]["e"]
                nc.scalar.activation(e[:], e[:], ACT.Exp).then_inc(att_exp[stage], 1)

            def turned1(g):
                bank, cols = TURN_BANK + g % 2, slice(g * S, g * S + S)
                act.wait_ge(tr_ready, g + 1)
                nc.scalar.activation(xnt_a[0][:, cols], ps[0:DA, bank, 0:S], ACT.Copy)
                nc.scalar.activation(xnt_b[0:DB, cols], ps[0:DB, bank, 128:128 + S], ACT.Copy).then_inc(xnt_hi_ready, 1)

            def split_wtok():
                for half_k in range(2):
                    act.wait_ge(wtok_loaded[half_k], 16)
                nc.scalar.activation(wtok_part[0][:], wtok[:], ACT.Copy).then_inc(wtok_hi, 1)

            def split_patches(c):
                act.wait_ge(x_loaded[c + 1], 16)
                nc.scalar.activation(x_part[0][:, c - 2], x[:, c], ACT.Copy).then_inc(x_part_hi, 1)

            def split_qkv(j):
                cols = slice(QKV_J * j, QKV_J * j + QKV_J)
                nc.scalar.activation(wqkv_hi[:, :, cols], wqkv[:, :, cols], ACT.Copy).then_inc(qkv_hi, 1)

            def turned2(g):
                copy_turned(g, tr2_ready, xn2t_a[:, g, :], xn2t_b[:, g, :], TURN_BANK + g % 2, xn2t_ready, g + 1)

            def norm_apply(p):
                act.wait_ge(ln_bias_ready, p - ACT_NORMS[0] + 1)
                for i in range(2):
                    g = 2 * (p % GH) + i
                    nc.scalar.activation(xn[:, g, :], h[:, g, :], ACT.Identity, bias=ln_bias[:, g:g + 1],
                                         scale=rstd[:, g:g + 1]).then_inc(xn_by_act, 1)

            def split_x(p):
                act.wait_ge(*normed(2 * p + 1, 1))
                gs = slice(2 * p, 2 * p + 2)
                nc.scalar.activation(x_hi[:, gs, 0:D], xn[:, gs, :], ACT.Copy)
                nc.scalar.activation(x_hi[:, gs, D:], xn[:, gs, DA:], ACT.Copy).then_inc(x_hi_ready, 1)

            def route_exps(half):
                act.wait_ge(route_shift, half + 1)
                gs = slice(GH * half, GH * half + GH)
                nc.scalar.activation(ex[:, gs, :], shifted[:, gs, :], ACT.Exp).then_inc(route_exp, 1)

            def slots_hi(g):
                act.wait_ge(ei_hi_psum, g + 1)
                nc.scalar.activation(slots_of(ei[0], g), dispatched(g, 0), ACT.Copy).then_inc(ei_hi_ready, 1)

            def slots_lo(g):
                act.wait_ge(ei_lo_psum, g + 1)
                nc.scalar.activation(slots_of(ei[1], g), dispatched(g, 1), ACT.Copy).then_inc(ei_lo_ready[0], 1)

            def split_in(e):
                act.wait_ge(wi_loaded[e % 2], 2 * 16 * (e // 2 + 1))
                if e >= 2:
                    act.wait_ge(hid_psum, 3 * (e - 1))
                nc.scalar.activation(w_b[e % 2][0:DB, :], raw_b[:, e % 2, :], ACT.Copy)
                nc.scalar.activation(w[e % 2][:, 0, 0:WO], raw[:, e % 2, 0:WO], ACT.Copy).then_inc(wi_hi, 1)

            def split_out(e):
                act.wait_ge(wo_loaded[e % 2], 16 * (e // 2 + 1))
                if e >= 2:
                    act.wait_ge(y_psum, e - 1)
                nc.scalar.activation(w[e % 2][:, 0, WO:WEXP], raw[:, e % 2, WO:WEXP], ACT.Copy).then_inc(wo_hi, 1)

            def hidden_hi(e, pairs=range(FT // 2)):
                for pair in pairs:
                    act.wait_ge(hid_psum, 3 * e + pair + 1)
                    if e >= 2 and pair == 0:
                        act.wait_ge(y_psum, e - 1)
                    nc.scalar.activation(h_hi[e % 2][:, 2 * pair:2 * pair + 2, :],
                                         ps[:, 3 * (e % 2) + pair, 0:2 * SLOTS].rearrange("p (t s) -> p t s", t=2),
                                         ACT.Relu).then_inc(hid_hi, 1)

            def turned_comb(half):
                act.wait_ge(combT_psum, half + 1)
                for s in range(2):
                    rows = (HS, HS - CAP)[s]
                    src = ps[0:rows, COMBT_BANK[half]:COMBT_BANK[half] + 2, :]
                    src = src.rearrange("p b (g e s) -> p b g e s", g=2, e=2)[:, :, :, s, 0:S]
                    dst = combT[0:rows, GH * half:GH * half + GH, s, :].rearrange("p (b g) s -> p b g s", b=2)
                    last = nc.scalar.activation(dst, src, ACT.Copy)
                last.then_inc(combT_ready, 1)

            def turned_comb7():
                act.wait_ge(comb7T_psum, 1)
                src = ps[0:HS, COMB7T_BANK:COMB7T_BANK + 2, :].rearrange("p b (g s) -> p b g s", g=GH)[:, :, :, 0:S]
                nc.scalar.activation(comb7T[:].rearrange("p (b g) s -> p b g s", b=2), src, ACT.Copy)\
                    .then_inc(comb7T_ready, 1)

            def low_y(e):
                act.wait_ge(y_psum, e + 1)
                if e >= 1:
                    act.wait_ge(y_held, e)
                nc.scalar.activation(y_low[:], y_banks(e)[:, :, D:2 * D], ACT.Copy).then_inc(y_low_held, 1)

            split_wtok()
            split_patches(2)
            act.wait_ge(wqkv_loaded, 16)
            for j in range(3):
                split_qkv(j)
            turned1(0)
            turned1(1)
            split_patches(3)
            turned1(2)
            turned1(3)
            split_in(0)
            hold("q", 0)
            hold("k", 0)
            att_exps(0, 0)
            turned1(4)
            turned1(5)
            norm_apply(3)
            hold("v", 0)
            turned1(6)
            turned1(7)
            att_exps(1, 0)
            split_out(0)
            hold("q", 1)
            hold("k", 1)
            att_exps(0, 1)
            hold("v", 1)
            split_in(1)
            att_exps(1, 1)
            norm_apply(4)
            turned2(0)
            turned2(1)
            split_x(0)
            norm_apply(5)
            split_x(1)
            turned2(2)
            turned2(3)
            turned2(4)
            turned2(5)
            route_exps(0)
            turned2(6)
            turned2(7)
            split_x(2)
            split_x(3)
            route_exps(1)
            for g in range(4):
                slots_hi(g)
                slots_lo(g)
            for g in range(4, 8):
                slots_hi(g)
            turned_comb(0)
            hidden_hi(0, (0,))
            turned_comb7()
            hidden_hi(0, (1,))
            turned_comb(1)
            hidden_hi(0, (2,))
            for e in range(E - 1):
                if e + 2 < E:
                    split_in(e + 2)
                hidden_hi(e + 1)
                split_out(e + 1)
                low_y(e)
            low_y(E - 1)

        @block.vector
        def _(dve):
            def norm_stats(p):
                g0 = 2 * (p % GH)
                for i in range(2):
                    (embedded, attended)[p // GH](g0 + i)
                for i in range(2):
                    dve.wait_ge(added, 2 * p + i + 1)
                    nc.vector.bn_stats(stats[:, g0 + i, :], h[:, g0 + i, :]).then_inc(ln_stats, 1)
                for i in range(2):
                    dve.wait_ge(ln_stats, 2 * p + i + 1)
                    nc.vector.bn_aggr(moments[:, g0 + i, :], stats[:, g0 + i, :]).then_inc(ln_moments, 1)

            def norm_apply(p):
                dve.wait_ge(ln_rstd, p + 1)
                for i in range(2):
                    g = 2 * (p % GH) + i
                    nc.vector.tensor_scalar(xn[:, g, :], h[:, g, :], moments[:, g, 0:1], rstd[:, g:g + 1],
                                            ALU.subtract, ALU.mult).then_inc(xn_by_dve, 1)

            def turned1(g):
                bank, cols = TURN_BANK + g % 2, slice(g * S, g * S + S)
                dve.wait_ge(xnt_hi_ready, g + 1)
                nc.vector.tensor_tensor(xnt_a[1][:, cols], ps[0:DA, bank, 0:S], xnt_a[0][:, cols].bitcast(F32), ALU.subtract)
                nc.vector.tensor_tensor(xnt_b[DB:128, cols], ps[0:DB, bank, 128:128 + S], xnt_b[0:DB, cols].bitcast(F32),
                                        ALU.subtract).then_inc(xnt_lo_ready, 1)

            def embedded(g):
                dve.wait_ge(tok_ready, g + 1)
                nc.vector.tensor_tensor(h[:, g, :], ps[0:S, EMBED_BANK + g % 2, 0:D], const("bias", S), ALU.add).then_inc(added, 1)

            def attended(g):
                dve.wait_ge(attn_out, g // 2 + 1)
                dve.wait_ge(biased, g // 2 + 1)
                bank = OUT_BANK[g // GH] + g % GH // 2
                nc.vector.tensor_tensor(h[:, g, :], ps[0:S, bank, g % 2 * D:g % 2 * D + D], h[:, g, :],
                                        ALU.add).then_inc(added, 1)

            def col(half, stage, n):
                return acol[:, half, stage, n, :]

            def softmax_shift(stage, half):
                lg, e = blocks(LOGIT_BANK[stage][half]), att[half]["e"]
                dve.wait_ge(att_logits[stage], half + 1)
                nc.vector.tensor_reduce(col(half, stage, 0).rearrange("p (b s) -> p b s", b=NB // 4), lg, AX.X,
                                        ALU.max).then_inc(att_max[stage], 1)
                dve.wait_ge(att_max[stage], half + 1)
                if stage == 1:
                    dve.wait_ge(att_weighted[0], half + 1)
                nc.vector.tensor_tensor(quads(e[:]), lg, spread(col(half, stage, 0)), ALU.subtract)\
                    .then_inc(att_shift[stage], 1)

            def softmax_sum(stage, half):
                dve.wait_ge(att_exp[stage], half + 1)
                nc.vector.tensor_reduce(col(half, stage, 1), att[half]["e"][:], AX.X, ALU.add).then_inc(att_sum[stage], 1)
                dve.wait_ge(att_sum[stage], half + 1)
                nc.vector.reciprocal(col(half, stage, 3), col(half, stage, 1)).then_inc(att_rsum[stage], 1)

            def softmax_mean(stage, half):
                dve.wait_ge(att_weighted[stage], half + 1)
                nc.vector.tensor_reduce(col(half, stage, 2), att[half]["w"][:], AX.X, ALU.add).then_inc(att_wsum[stage], 1)
                dve.wait_ge(att_wsum[stage], half + 1)
                dve.wait_ge(att_rsum[stage], half + 1)
                nc.vector.tensor_tensor(col(half, stage, 4), col(half, stage, 2), col(half, stage, 3), ALU.mult)\
                    .then_inc(att_glob[stage], 1)
                dve.wait_ge(att_glob[stage], half + 1)
                src, done = (("k", kq_ready), ("v", u_ready))[stage]
                dve.wait_ge(proj_held[src], half + 1)
                nc.vector.tensor_tensor(quads(att[half]["w"][:]), quads(att[half][src][:]),
                                        spread(col(half, stage, 4)), ALU.mult).then_inc(done, 1)

            steps = [0]

            def step(ins):
                steps[0] += 1
                ins.then_inc(route_step, 1)
                dve.wait_ge(route_step, steps[0])

            def per_group(c):
                return c.unsqueeze(2).broadcast_to([S, GH, E])

            def route_shifts(half):
                gs = slice(GH * half, GH * half + GH)
                lg = ps[0:S, OUT_BANK[half], 0:GH * E].rearrange("p (g e) -> p g e", g=GH)
                dve.wait_ge(router_ready, 2 * (half + 1))
                step(nc.vector.tensor_reduce(cols[:, half, 0, :], lg, AX.X, ALU.max))
                nc.vector.tensor_tensor(shifted[:, gs, :], lg, per_group(cols[:, half, 0, :]), ALU.subtract)\
                    .then_inc(route_shift, 1)

            def flat(t):
                return t.rearrange("p g e -> p (g e)")

            def route_first(half):
                gs = slice(GH * half, GH * half + GH)
                rank = const("rank", S)
                rank3 = rank.rearrange("p (g e) -> p g e", g=GH)
                first = chosen[:, half, 0, :].rearrange("p (g e) -> p g e", g=GH)
                dve.wait_ge(route_exp, half + 1)
                step(nc.vector.scalar_tensor_tensor(flat(ranked[:, gs, :]), flat(ex[:, gs, :]), 1.0, rank, ALU.is_ge, ALU.mult))
                step(nc.vector.tensor_reduce(cols[:, half, 3, :], ranked[:, gs, :], AX.X, ALU.max))
                nc.vector.tensor_tensor(first, rank3, per_group(cols[:, half, 3, :]), ALU.is_equal).then_inc(first_ready, 1)
                nc.vector.tensor_reduce(cols[:, half, 1, :], ex[:, gs, :], AX.X, ALU.add)

            def route_second(half):
                gs = slice(GH * half, GH * half + GH)
                rank3 = const("rank", S).rearrange("p (g e) -> p g e", g=GH)
                second = chosen[:, half, 1, :].rearrange("p (g e) -> p g e", g=GH)
                dve.wait_ge(first_ready, half + 1)
                step(nc.vector.scalar_tensor_tensor(flat(ex2[:, gs, :]), chosen[:, half, 0, :], -2.0, flat(ex[:, gs, :]),
                                                    ALU.mult, ALU.add))
                step(nc.vector.tensor_reduce(cols[:, half, 4, :], ex2[:, gs, :], AX.X, ALU.max))
                step(nc.vector.tensor_tensor(ranked2[:, gs, :], ex2[:, gs, :], per_group(cols[:, half, 4, :]), ALU.is_equal))
                step(nc.vector.tensor_tensor(ranked[:, gs, :], ranked2[:, gs, :], rank3, ALU.mult))
                step(nc.vector.tensor_reduce(cols[:, half, 5, :], ranked[:, gs, :], AX.X, ALU.max))
                nc.vector.tensor_tensor(second, rank3, per_group(cols[:, half, 5, :]), ALU.is_equal).then_inc(choice_ready, 1)
                nc.vector.reciprocal(cols[:, half, 2, :], cols[:, half, 1, :]).then_inc(rsum_ready, 1)

            def route_slots(half):
                dve.wait_ge(choice_ready, half + 1)
                dve.wait_ge(cum_ready, half + 1)
                cum = ps[0:S, OUT_BANK[half] + 1, 0:2 * GH * E]
                nc.vector.tensor_tensor(slot2[:, half].rearrange("p c n -> p (c n)"), chosen[:, half].rearrange("p c n -> p (c n)"),
                                        cum, ALU.mult).then_inc(cum_used, 1)
                dve.wait_ge(cum_used, half + 1)
                nc.vector.tensor_tensor(slot[:, half, :], slot2[:, half, 0, :], slot2[:, half, 1, :], ALU.add).then_inc(slot_ready, 1)

            def one_hot(p):
                half, n = p // 2, 2 * E
                if p % 2 == 0:
                    dve.wait_ge(slot_ready, half + 1)
                at = p % 2 * n
                nc.vector.tensor_tensor(
                    disp[:, 2 * p:2 * p + 2, :].rearrange("p g (e c) -> p (g e) c", e=E),
                    slot[:, half, at:at + n].unsqueeze(2).broadcast_to([S, n, CAP]),
                    const("iota", S).unsqueeze(1).broadcast_to([S, n, CAP]), ALU.is_equal).then_inc(disp_ready, 1)

            def slots_lo(g):
                dve.wait_ge(ei_lo_psum, g + 1)
                nc.vector.tensor_copy(slots_of(ei[1], g), dispatched(g, 1)).then_inc(ei_lo_ready[1], 1)

            def hidden_lo(e):
                for pair in range(FT // 2):
                    dve.wait_ge(hid_hi, 3 * e + pair + 1)
                    if e >= 2 and pair == 0:
                        dve.wait_ge(y_psum, e - 1)
                    nc.vector.scalar_tensor_tensor(
                        h_lo[e % 2][:, 2 * pair:2 * pair + 2, :].rearrange("p t s -> p (t s)"),
                        ps[:, 3 * (e % 2) + pair, 0:2 * SLOTS], 0.0,
                        h_hi[e % 2][:, 2 * pair:2 * pair + 2, :].rearrange("p t s -> p (t s)").bitcast(F32),
                        ALU.max, ALU.subtract).then_inc(hid_lo, 1)

            def split_patches(c):
                dve.wait_ge(x_part_hi, c - 1)
                nc.vector.tensor_tensor(x_part[1][:, c - 2], x[:, c], x_part[0][:, c - 2].bitcast(F32),
                                        ALU.subtract).then_inc(x_part_lo, 1)

            def split_in_b(e):
                dve.wait_ge(wi_hi, e + 1)
                nc.vector.tensor_tensor(w_b[e % 2][DB:128, :], raw_b[:, e % 2, :], w_b[e % 2][0:DB, :].bitcast(F32),
                                        ALU.subtract).then_inc(wi_b_lo, 1)

            def hold_y(e):
                dve.wait_ge(y_low_held, e + 1)
                if e >= 2:
                    dve.wait_ge(y_moved[e % 2], 16 * GH * (e // 2))
                nc.vector.tensor_tensor(y[:, e % 2], y_banks(e)[:, :, 0:D], y_low[:], ALU.add).then_inc(y_held, 1)

            nc.vector.memset(filler[:], 1.0).then_inc(filler_ready, 1)
            dve.wait_ge(small_loaded, 16)
            at = SMALL["wqk"][0]
            for j in range(4):
                nc.vector.tensor_scalar(blk[:, j, :], const("mask"), small[:, at + j:at + j + 1], SCALE, ALU.mult,
                                        ALU.mult).then_inc(blk_ready, 1)
            norm_stats(0)
            split_patches(2)
            norm_apply(0)
            norm_stats(1)
            turned1(0)
            turned1(1)
            norm_apply(1)
            turned1(2)
            turned1(3)
            split_patches(3)
            norm_stats(2)
            norm_apply(2)
            split_in_b(0)
            softmax_shift(0, 0)
            norm_stats(3)
            softmax_sum(0, 0)
            turned1(4)
            turned1(5)
            softmax_mean(0, 0)
            turned1(6)
            turned1(7)
            softmax_shift(1, 0)
            softmax_sum(1, 0)
            softmax_mean(1, 0)
            softmax_shift(0, 1)
            softmax_sum(0, 1)
            softmax_mean(0, 1)
            norm_stats(4)
            softmax_shift(1, 1)
            norm_stats(5)
            softmax_sum(1, 1)
            softmax_mean(1, 1)
            dve.wait_ge(tables_loaded, 16)
            nc.vector.tensor_copy(tri[:], const("tri", S)).then_inc(cast_ready, 1)
            nc.vector.tensor_copy(ones[:], const("ones", S)).then_inc(cast_ready, 1)
            norm_stats(6)
            norm_stats(7)
            norm_apply(6)
            route_shifts(0)
            norm_apply(7)
            route_first(0)
            route_second(0)
            route_shifts(1)
            route_slots(0)
            one_hot(0)
            route_first(1)
            route_second(1)
            one_hot(1)
            route_slots(1)
            one_hot(2)
            one_hot(3)
            for g in range(4, 8):
                slots_lo(g)
            split_in_b(1)
            hidden_lo(0)
            for e in range(E):
                if e + 2 < E:
                    split_in_b(e + 2)
                if e + 1 < E:
                    hidden_lo(e + 1)
                hold_y(e)
            for p in range(4):
                dve.wait_ge(mix_psum, p + 1)
                nc.vector.tensor_tensor(res[:, 2 * p:2 * p + 2, :],
                                        ps[0:S, MIX_BANK + p, :].rearrange("p (g d) -> p g d", g=2)[:, :, 0:D],
                                        h[:, 2 * p:2 * p + 2, :], ALU.add).then_inc(res_ready, 1)

        @block.gpsimd
        def _(pool):
            def inverse_std(p):
                gs = slice(2 * (p % GH), 2 * (p % GH) + 2)
                pool.wait_ge(ln_moments, 2 * p + 2)
                nc.gpsimd.tensor_tensor(var[:, gs], moments[:, gs, 1], const("eps", S), ALU.add).then_inc(ln_var, 1)
                if p in ACT_NORMS:
                    nc.gpsimd.tensor_tensor(minus_mean[:, gs], moments[:, gs, 0], const("minus", S), ALU.mult).then_inc(ln_minus, 1)
                pool.wait_ge(ln_var, p + 1)
                nc.gpsimd.tensor_tensor(rstd[:, gs], var[:, gs], const("power", S), ALU.pow).then_inc(ln_rstd, 1)
                if p in ACT_NORMS:
                    pool.wait_ge(ln_minus, p - ACT_NORMS[0] + 1)
                    pool.wait_ge(ln_rstd, p + 1)
                    nc.gpsimd.tensor_tensor(ln_bias[:, gs], minus_mean[:, gs], rstd[:, gs], ALU.mult).then_inc(ln_bias_ready, 1)

            def weigh(stage, half):
                pool.wait_ge(att_exp[stage], half + 1)
                src = "qk"[stage]
                pool.wait_ge(proj_held[src], half + 1)
                if stage == 1:
                    pool.wait_ge(att_logits[1], half + 1)
                nc.gpsimd.tensor_tensor(att[half]["w"][:], att[half]["e"][:], att[half][src][:], ALU.mult)\
                    .then_inc(att_weighted[stage], 1)

            def split_qkv(j):
                cols = slice(QKV_J * j, QKV_J * j + QKV_J)
                pool.wait_ge(qkv_hi, j + 1)
                nc.gpsimd.tensor_tensor(wqkv_lo[:, :, cols], wqkv[:, :, cols], wqkv_hi[:, :, cols].bitcast(F32),
                                        ALU.subtract).then_inc(qkv_lo, 1)

            def bias(p):
                pool.wait_ge(*normed(2 * p + 1, 0))
                gs = slice(2 * p, 2 * p + 2)
                nc.gpsimd.tensor_tensor(h[:, gs, :], h[:, gs, :], const("bp", S).unsqueeze(1).broadcast_to([S, 2, D]),
                                        ALU.add).then_inc(biased, 1)

            def split(e, hi, done, a, b):
                pool.wait_ge(hi, e + 1)
                nc.gpsimd.tensor_tensor(w[e % 2][:, 1, a:b], raw[:, e % 2, a:b], w[e % 2][:, 0, a:b].bitcast(F32),
                                        ALU.subtract).then_inc(done, 1)

            def split_in(e):
                split(e, wi_hi, wi_lo, 0, WO)

            def split_out(e):
                split(e, wo_hi, wo_lo, WO, WEXP)

            def split_x(p):
                pool.wait_ge(x_hi_ready, p + 1)
                gs = slice(2 * p, 2 * p + 2)
                nc.gpsimd.tensor_tensor(x_lo[:, gs, 0:D], xn[:, gs, :], x_hi[:, gs, 0:D].bitcast(F32), ALU.subtract)
                nc.gpsimd.tensor_tensor(x_lo[:, gs, D:], xn[:, gs, DA:], x_hi[:, gs, D:].bitcast(F32), ALU.subtract)\
                    .then_inc(x_lo_ready, 1)

            def gates(half):
                gs = slice(GH * half, GH * half + GH)
                n = GH * E
                pool.wait_ge(rsum_ready, half + 1)
                pool.wait_ge(choice_ready, half + 1)
                nc.gpsimd.tensor_tensor(gate[:, half, 0, :], chosen[:, half, 0, :], chosen[:, half, 1, :], ALU.add)\
                    .then_inc(gate_step, 1)
                nc.gpsimd.tensor_tensor(gate[:, half, 1, :].rearrange("p (g e) -> p g e", g=GH), ex[:, gs, :],
                                        cols[:, half, 2, :].unsqueeze(2).broadcast_to([S, GH, E]), ALU.mult)\
                    .then_inc(gate_step, 1)
                pool.wait_ge(gate_step, 3 * half + 2)
                nc.gpsimd.tensor_tensor(gate[:, half, 2, :], gate[:, half, 0, :], gate[:, half, 1, :], ALU.mult)\
                    .then_inc(gate_step, 1)
                pool.wait_ge(gate_step, 3 * half + 3)
                pool.wait_ge(disp_ready, 2 * half + 2)
                nc.gpsimd.tensor_tensor(comb[:, gs, :].rearrange("p g (e c) -> p (g e) c", e=E),
                                        disp[:, gs, :].rearrange("p g (e c) -> p (g e) c", e=E).bitcast(F32),
                                        gate[:, half, 2, :].unsqueeze(2).broadcast_to([S, n, CAP]), ALU.mult)\
                    .then_inc(comb_ready, 1)
                own = comb7[:, half, :].rearrange("p (g n) -> p g n", g=GH)[:, :, 0:CAP]
                last_gate = gate[:, half, 2, :].rearrange("p (g e) -> p g e", g=GH)[:, :, E - 1:E]
                nc.gpsimd.tensor_tensor(own, disp[:, gs, EC - CAP:EC].bitcast(F32), last_gate.broadcast_to([S, GH, CAP]),
                                        ALU.mult).then_inc(comb7_ready, 1)

            nc.gpsimd.memset(comb7[:], 0.0).then_inc(comb7_zero, 1)
            pool.wait_ge(comb7_zero, 1)
            pool.wait_ge(small_loaded, 16)
            pool.wait_ge(wtok_hi, 1)
            nc.gpsimd.tensor_tensor(wtok_part[1][:], wtok[:], wtok_part[0][:].bitcast(F32), ALU.subtract).then_inc(wtok_lo, 1)
            inverse_std(0)
            split_qkv(0)
            inverse_std(1)
            split_qkv(1)
            split_qkv(2)
            inverse_std(2)
            pool.wait_ge(tables_loaded, 16)
            bias(0)
            bias(1)
            weigh(0, 0)
            inverse_std(3)
            bias(2)
            weigh(1, 0)
            bias(3)
            split_in(0)
            weigh(0, 1)
            split_out(0)
            inverse_std(4)
            weigh(1, 1)
            inverse_std(5)
            split_x(0)
            inverse_std(6)
            inverse_std(7)
            split_x(1)
            split_in(1)
            split_x(2)
            split_x(3)
            gates(0)
            gates(1)
            for e in range(E - 1):
                if e + 2 < E:
                    split_in(e + 2)
                split_out(e + 1)


def kernel(**inputs):
    import concourse.bacc as _bacc
    from concourse.bass_utils import run_bass_kernel_spmd as _run

    a = {k: np.asarray(v) for k, v in inputs.items()}
    f32 = np.float32

    xi = a["x"].reshape(IMAGES, 3, 7, 16, 7, 16).transpose(3, 5, 1, 0, 2, 4).reshape(KT, 128, 4, 2 * S)
    xi = np.ascontiguousarray(xi.transpose(2, 1, 0, 3)).reshape(4, 128, KT * 2 * S)
    wt = np.ascontiguousarray(a["L0_tok_W_lin"].T.reshape(KT, 128, D).transpose(1, 0, 2)).reshape(128, KT * D)

    wq = a["L0_attn_Wqkv"].T
    wqkv = np.zeros((128, 2, QKV_W), f32)
    for k, rows in enumerate((slice(0, DA), slice(DA, D))):
        n = rows.stop - rows.start
        for j in range(3):
            at = QKV_J * j
            wqkv[:n, k, at:at + DA] = wq[rows, D * j:D * j + DA]
            wqkv[:n, k, at + DA + DB:at + DA + 2 * DB] = wq[rows, D * j + DA:D * j + D]
    wqkv[DB:, 1] = wqkv[:DB, 1]

    small = np.zeros((128, SMALL_W), f32)

    def put(name, value):
        at, w = SMALL[name]
        value = np.asarray(value)
        small[:value.shape[0], at:at + w] = value

    put("bias", np.broadcast_to(a["L0_tok_b_lin"], (128, D)))
    head = np.arange(128) // HD
    put("bp", np.broadcast_to(a["L0_attn_bp"], (128, D)))
    put("mask", (head[:, None] == head[None, :]).astype(f32))
    wqv, wkv = a["L0_attn_w_q"].reshape(D), a["L0_attn_w_k"].reshape(D)
    put("wqk", np.stack([wqv[:DA], np.tile(wqv[DA:], 2), wkv[:DA], np.tile(wkv[DA:], 2)], axis=1))
    put("ident", np.eye(128, dtype=f32))
    wp = a["L0_attn_Wp"].T
    put("wp_a", wp[:DA])
    put("wp_b", np.concatenate([wp[DA:], wp[DA:]]))
    put("router_a", a["L0_ffn_w_router"][:DA])
    put("router_b", a["L0_ffn_w_router"][DA:])
    put("tri", np.triu(np.ones((S, S), f32)))
    put("ones", np.ones((S, S), f32))
    put("rank", np.broadcast_to(np.tile(E - np.arange(E, dtype=f32), GH), (S, GH * E)))
    put("iota", np.broadcast_to(np.arange(1, CAP + 1, dtype=f32), (S, CAP)))

    put("eps", np.full((S, 2), EPS, f32))
    put("power", np.full((S, 2), -0.5, f32))
    put("minus", np.full((S, 2), -1.0, f32))

    wi, wo = a["L0_ffn_wi"], a["L0_ffn_wo"]
    wexp = np.empty((E, 128, WEXP), f32)
    wexp[:, :, 0:F] = wi[:, :DA]
    wexp[:, :, WO:] = wo.reshape(E, FT, 128, D).transpose(0, 2, 1, 3).reshape(E, 128, FT * D)
    wexp_b = np.ascontiguousarray(wi[:, DA:])

    arrays = {"x_dram": xi, "wtok_dram": wt, "wqkv_dram": wqkv.reshape(128, 2 * QKV_W), "small_dram": small,
              "wexp_dram": wexp, "wexp_b_dram": wexp_b}
    nc = _bacc.Bacc("TRN2", target_bir_lowering=False, num_devices=1)
    args = [nc.dram_tensor(k, v.shape, F32, kind="ExternalInput").ap() for k, v in arrays.items()]
    out = nc.dram_tensor("out_0_dram", (IMAGES * N_TOK, D), F32, kind="ExternalOutput").ap()
    build(nc, *args, out)
    r = _run(nc, [arrays], core_ids=[0])
    return r.results[0]["out_0_dram"].reshape(IMAGES, N_TOK, D)
```
